# Optimizing a Trainium2 kernel written in Bass

```python
import numpy as np
import jax
import jax.numpy as jnp

def _softmax(x, axis=-1):
    return jax.nn.softmax(x, axis=axis)

def _gelu(x):
    return jax.nn.gelu(x, approximate=True)

def _silu(x):
    return jax.nn.silu(x)

def _sigmoid(x):
    return jax.nn.sigmoid(x)

def _layernorm(x, axis=-1, eps=1e-05):
    m = jnp.mean(x, axis=axis, keepdims=True)
    v = jnp.var(x, axis=axis, keepdims=True)
    return (x - m) / jnp.sqrt(v + eps)

def _scatter_add(tgt, idx, src, axis=0):
    return tgt.at[idx].add(src)

def _segment_sum(src, seg, n):
    return jax.ops.segment_sum(src, seg, n)
kernel_name = 'mk_gnn_preln_d2_gnn_r32_f064cd'

def setup_inputs(seed: int=0):
    np.random.seed(seed)
    _w = jnp.asarray

    def _rec_inputs():
        import jax
        import jax.numpy as jnp
        _gk = jax.random.key(seed)
        x = -0.0005121 + 1.001 * jax.random.normal(jax.random.fold_in(_gk, 1), (3125, 64), jnp.float32)
        _s = jax.random.randint(jax.random.fold_in(_gk, 2), (50000,), 0, 3125, jnp.int32)
        _d = jax.random.randint(jax.random.fold_in(_gk, 3), (50000,), 0, 3125, jnp.int32)
        _loop = jnp.arange(3125, dtype=jnp.int32)
        src = jnp.concatenate([_s, _d, _loop])
        dst = jnp.concatenate([_d, _s, _loop])
        _o = jnp.argsort(dst, stable=True)
        src = src[_o]
        dst = dst[_o]
        edge_attr_64 = -4.21973e-05 + 0.999841 * jax.random.normal(jax.random.fold_in(_gk, 11), (103125, 64), jnp.float32)
        return (x, src, dst, edge_attr_64)
    x, src, dst, edge_attr_64 = _rec_inputs()

    def _L0_gnn_setup():
        import jax, jax.numpy as jnp
        import numpy as np
        N = 50000
        E = 37500
        NODE_DIM = 64
        EDGE_DIM = 64
        key = jax.random.key(seed)
        ks = jax.random.split(key, 10)
        h = jax.random.normal(ks[0], (N, NODE_DIM), dtype=jnp.float32)
        e = jax.random.normal(ks[1], (E, EDGE_DIM), dtype=jnp.float32)
        edge_index = jax.random.randint(ks[2], (2, E), 0, N, dtype=jnp.int64)
        s1 = 1.0 / np.sqrt(NODE_DIM + EDGE_DIM)
        W1 = jax.random.uniform(ks[3], (NODE_DIM + EDGE_DIM, NODE_DIM), jnp.float32, -s1, s1)
        b1 = jax.random.uniform(ks[4], (NODE_DIM,), jnp.float32, -s1, s1)
        s2 = 1.0 / np.sqrt(NODE_DIM)
        W2 = jax.random.uniform(ks[5], (NODE_DIM, NODE_DIM), jnp.float32, -s2, s2)
        b2 = jax.random.uniform(ks[6], (NODE_DIM,), jnp.float32, -s2, s2)
        s3 = 1.0 / np.sqrt(2 * NODE_DIM)
        W3 = jax.random.uniform(ks[7], (2 * NODE_DIM, NODE_DIM), jnp.float32, -s3, s3)
        b3 = jax.random.uniform(ks[8], (NODE_DIM,), jnp.float32, -s3, s3)
        return {'h': h, 'e': e, 'W1': W1, 'b1': b1, 'W2': W2, 'b2': b2, 'W3': W3, 'b3': b3, 'edge_index': edge_index}
    _L0_gnn_all = _L0_gnn_setup()
    _L0_gnn_in = {k: v for k, v in _L0_gnn_all.items() if k in ('W1', 'b1', 'W2', 'b2', 'W3', 'b3')}
    del _L0_gnn_all

    def _L1_gnn_setup():
        import jax, jax.numpy as jnp
        import numpy as np
        NUM_USERS = 3125
        NUM_MOVIES = 50000
        NUM_NODES = NUM_USERS + NUM_MOVIES
        EMB_DIM = 64
        N_LAYERS = 3
        N_EDGES = 125000
        key = jax.random.key(seed)
        k_e, k_w = jax.random.split(key)
        edge_index = jax.random.randint(k_e, (2, N_EDGES), 0, NUM_NODES, dtype=jnp.int64 if jax.config.jax_enable_x64 else jnp.int32)
        emb_weight = jax.random.normal(k_w, (NUM_NODES, EMB_DIM), dtype=jnp.float32)
        return {'edge_index': edge_index, 'emb_weight': emb_weight}
    _L1_gnn_all = _L1_gnn_setup()
    _L1_gnn_in = {k: v for k, v in _L1_gnn_all.items() if k in ()}
    del _L1_gnn_all
    return {'x': x, 'src': src, 'dst': dst, 'edge_attr_64': edge_attr_64, 'L0_gnn_W1': _L0_gnn_in['W1'], 'L0_gnn_b1': _L0_gnn_in['b1'], 'L0_gnn_W2': _L0_gnn_in['W2'], 'L0_gnn_b2': _L0_gnn_in['b2'], 'L0_gnn_W3': _L0_gnn_in['W3'], 'L0_gnn_b3': _L0_gnn_in['b3']}

def reference(x, src, dst, edge_attr_64, L0_gnn_W1, L0_gnn_b1, L0_gnn_W2, L0_gnn_b2, L0_gnn_W3, L0_gnn_b3):
    import jax
    import jax.numpy as jnp

    def _L0_gnn_ref(h, e, W1, b1, W2, b2, W3, b3, edge_index):
        import jax, jax.numpy as jnp
        import numpy as np
        N = 50000
        E = 37500
        NODE_DIM = 64
        EDGE_DIM = 64
        src, dst = (edge_index[0], edge_index[1])
        msg_input = jnp.concatenate([h[src], e], axis=-1)
        hidden = jax.nn.relu(msg_input @ W1 + b1)
        messages = hidden @ W2 + b2
        agg = jax.ops.segment_sum(messages, dst, num_segments=h.shape[0])
        h_new = jax.nn.relu(jnp.concatenate([h, agg], axis=-1) @ W3 + b3)
        return h_new

    def _L1_gnn_ref(edge_index, emb_weight):
        import jax, jax.numpy as jnp
        import numpy as np
        NUM_USERS = 3125
        NUM_MOVIES = 50000
        NUM_NODES = NUM_USERS + NUM_MOVIES
        EMB_DIM = 64
        N_LAYERS = 3
        N_EDGES = 125000
        row, col = (edge_index[0], edge_index[1])
        num_nodes = emb_weight.shape[0]
        deg = jax.ops.segment_sum(jnp.ones_like(col, dtype=emb_weight.dtype), col, num_segments=num_nodes)
        deg_inv_sqrt = jnp.where(deg > 0, jax.lax.rsqrt(jnp.maximum(deg, 1.0)), 0.0)
        deg_inv_sqrt = jnp.where(deg > 0, deg ** (-0.5), 0.0)
        norm = deg_inv_sqrt[row] * deg_inv_sqrt[col]
        embs = emb_weight
        acc = emb_weight
        for _ in range(N_LAYERS):
            msgs = norm[:, None] * embs[row]
            embs = jax.ops.segment_sum(msgs, col, num_segments=num_nodes)
            acc = acc + embs
        return acc / (N_LAYERS + 1)
    edge_index = jnp.stack([src, dst])
    h = jnp.maximum(_layernorm(x, axis=-1), 0.0)
    x = x + _L0_gnn_ref(h, edge_attr_64, L0_gnn_W1, L0_gnn_b1, L0_gnn_W2, L0_gnn_b2, L0_gnn_W3, L0_gnn_b3, edge_index)
    h = jnp.maximum(_layernorm(x, axis=-1), 0.0)
    x = x + _L1_gnn_ref(edge_index, h)
    return x

_drawn_inputs = setup_inputs


def setup_inputs(seed=0):
    import zlib

    import numpy as np

    out = dict(_drawn_inputs(seed))
    spreads = {}
    factors = {'L0_gnn_b3': 2.929}
    for name, (base, spread) in spreads.items():
        noise = np.random.default_rng([zlib.crc32(name.encode()), seed]).standard_normal(out[name].shape)
        drawn = base * np.exp(spread * noise) if base else spread * noise
        out[name] = jnp.asarray(drawn.astype(out[name].dtype))
    for name, factor in factors.items():
        out[name] = (out[name] * factor).astype(out[name].dtype)
    return out
```

```python
from contextlib import ExitStack

import concourse.bass as bass
from concourse import mybir

ALU = mybir.AluOpType
ACT = mybir.ActivationFunctionType
AX = mybir.AxisListType
F32 = mybir.dt.float32
F16 = mybir.dt.float16
BF16 = mybir.dt.bfloat16
I32 = mybir.dt.int32

P = 128
F = 64
W = 16
HALF = 3
BODY = 2 * HALF
MAX_EXACT = 256
FAR = 1 << 20
NO_SLOT = 1000.0
EPS = 1e-5
BLK_BANK = 4
DST_BODY = 5


def gnn_and_propagation(nc, x, src, dst, edge, W1, b1, W2, b2, W3, b3, out):
    N, E = x.shape[0], src.shape[0]
    NB = -(-N // P)
    NPAD = NB * P
    NLAST = N - (NB - 1) * P
    GE = 2 * P
    NG = -(-E // GE)
    NFULL = E // GE
    TAIL = E - NFULL * GE
    RB = -(-NG // P)
    RLAST = NFULL - (RB - 1) * P
    KEYS = NB * W
    assert NFULL % BODY == 0 and NG == NFULL + 1 and TAIL > P and NB % DST_BODY == 0

    with ExitStack() as ctx:
        def sb(name, shape, dt, stack=ctx):
            return stack.enter_context(nc.sbuf_tensor(name, shape, dt))

        def sem(name):
            return ctx.enter_context(nc.semaphore(name))

        P_dram = nc.dram_tensor("node_part", (NPAD, F), F32).ap()
        y3_dram = nc.dram_tensor("node_update", (NPAD, F), F32).ap()
        U_dram = nc.dram_tensor("scaled", (NPAD, F), F32).ap()

        A = sb("A", [P, NB, NPAD], BF16)

        def slab(q, n=1, dt=F32):
            return A[:, q:q + n, :].rearrange("p a b -> p (a b)").bitcast(dt)

        ZEROED_EARLY = 12
        h_s = slab(12)
        sq_s = slab(13)
        Pn_s = slab(14)
        hT = slab(15, 2)
        x_s = slab(17)
        qr_s = slab(18)[:, 0:RB * GE]
        srcf_s = slab(19)[:, 0:RB * GE]
        rf_s = slab(20)[:, 0:RB * GE]
        key_s = slab(21)[:, 0:RB * GE]
        dl_s = slab(22)[:, 0:RB * GE]
        dst_s = slab(23, 1, I32)[:, 0:RB * GE]
        src_s = slab(24, 1, I32)[:, 0:RB * GE]
        ri_s = slab(13, 1, I32)[:, 0:RB * GE]

        F1 = F + 1
        node3 = lambda t: t.rearrange("p (b f) -> p b f", f=F)
        x2_g, acc_g, y3_g, sq_g, u_g = (node3(slab(q)) for q in (0, 1, 2, 12, 13))
        sums_g = slab(3, 2)[:, 0:NB * F1].rearrange("p (b c) -> p b c", c=F1)
        iota_g = slab(5, 2)
        oh_g = slab(7, 4).rearrange("p (g n) -> p g n", g=2)
        small_g = slab(11)
        e_g = small_g[:, 0:2 * F].rearrange("p (g f) -> p g f", g=2)
        got_g = small_g[:, 2 * F:4 * F].rearrange("p (g f) -> p g f", g=2)
        eT_g = small_g[:, 4 * F:6 * F]
        pre_g = small_g[:, 6 * F:8 * F].rearrange("p (g f) -> p g f", g=2)
        rows_g = small_g[:, 8 * F:8 * F + 2 * F1].rearrange("p (g c) -> p g c", g=2)
        dstf_g = small_g[:, 12 * F:12 * F + 2]
        src_g = slab(11, 1, I32)[:, 13 * F:13 * F + 2]
        dst_g = slab(11, 1, I32)[:, 14 * F:14 * F + 2]

        ident = sb("ident", [P, P], F32)
        ones = sb("ones", [P, 1], F32)
        W1n = sb("W1n", [F + 1, 2 * F], F32)
        W1e = sb("W1e", [P, P], F32)
        W2b = sb("W2b", [F + 1, F], F32)
        W2T = sb("W2T", [F, F + 1], F32)
        W3a = sb("W3a", [F, F], F32)
        W23 = sb("W23", [F + 1, F + 1], F32)
        stat = sb("stat", [P, 6, NB], F32)
        mean, var, std, rstd, deg, dis = (stat[:, i, :] for i in range(6))
        epst = sb("epst", [P, 1], F32)
        unfit = sb("unfit", [P, 2], F32)
        flag = sb("flag", [1, 1], I32)
        base_n = sb("base_n", [P, RB], F32)
        base_row = sb("base_row", [1, RB * P], I32)
        y3 = sb("y3", [P, NB, F], F32)
        aggT = sb("aggT", [F + 1, NPAD], F32)

        edge_phase = ExitStack()
        eb = lambda name, shape, dt: sb(name, shape, dt, edge_phase)
        srcT = eb("srcT", [P, NG, 2], I32)
        keyT = eb("keyT", [P, NG, 2], F32)
        rT = eb("rT", [P, NG, 2], F32)
        dlT = eb("dlT", [P, NG, 2], F32)
        iota_key = eb("iota_key", [P, KEYS], F16)
        iota_r = eb("iota_r", [P, P], BF16)
        iota_w = eb("iota_w", [P, W], F32)
        e_ring = eb("e_ring", [P, BODY, 2, F], F32)
        g_ring = eb("g_ring", [P, BODY, 2, F], F32)
        gidx = eb("gidx", [P, 2, HALF, 2], I32)
        eT = eb("eT", [P, 2, P], F32)
        pre = eb("pre", [P, 2, 2, F], F32)
        hid = eb("hid", [P, 2, 2, F + 1], F32)
        oh_key = eb("oh_key", [P, 2, 2, KEYS], BF16)
        oh_r = eb("oh_r", [P, 2, 2, P], BF16)
        oh_w = eb("oh_w", [P, 2, 2, W], F32)
        edge_phase.close()

        prop_phase = ExitStack()
        pb = lambda name, shape, dt: sb(name, shape, dt, prop_phase)
        U = pb("U", [P, 2, NB, 3, F], BF16)
        acc = pb("acc", [P, NB, F], F32)
        v = pb("v", [P, DST_BODY, F], F32)
        u = pb("u", [P, DST_BODY, F], F32)
        prop_phase.close()
        big = U[:, :, :, :, :].rearrange("p a b c d -> p (a b c d)").bitcast(F32)
        x_r = big[:, 0:NB * F].rearrange("p (b f) -> p b f", f=F)
        sq_r = big[:, NB * F:2 * NB * F].rearrange("p (b f) -> p b f", f=F)

        ps = [ctx.enter_context(nc.psum_tensor(f"ps{i}", [P, 512], F32)) for i in range(8)]
        ps_eT, ps_H, ps_A, ps_G = ps[0:2], ps[2:4], ps[4:6], ps[6:8]

        padded = sem("padded")
        x_in, idx_in, w_in, xr_in = sem("x_in"), sem("idx_in"), sem("w_in"), sem("xr_in")
        consts = sem("consts")
        cleared0 = sem("cleared0")
        filled = sem("filled")
        link_d = sem("link_d")
        ln_var, ln_std = sem("ln_var"), sem("ln_std")
        h_done = sem("h_done")
        hT_ps, hT_sb = sem("hT_ps"), sem("hT_sb")
        nodes_ps, nodes_ps_read, nodes_sb = sem("nodes_ps"), sem("nodes_ps_read"), sem("nodes_sb")
        base_read = sem("base_read")
        P_out, y3_out = sem("P_out"), sem("y3_out")
        nat_done = sem("nat_done")
        turned, turned_sb = sem("turned"), sem("turned_sb")
        wfold_ps, wfold_sb = sem("wfold_ps"), sem("wfold_sb")
        e_in = [sem(f"e_in{i}") for i in range(2)]
        gidx_done, gidx_seen = sem("gidx_done"), sem("gidx_seen")
        gathered = [sem(f"gathered{i}") for i in range(BODY)]
        eT_ps, eT_sb = sem("eT_ps"), sem("eT_sb")
        H_ps = sem("H_ps")
        pre_done, hid_done = sem("pre_done"), sem("hid_done")
        onehots = sem("onehots")
        A_ps, A_added = sem("A_ps"), sem("A_added")
        G_ps, G_added = sem("G_ps"), sem("G_added")
        z_ps = sem("z_ps")
        deg_done, sqrt_done = sem("deg_done"), sem("sqrt_done")
        U_done = sem("U_done")
        V_ps, V_read = sem("V_ps"), sem("V_read")
        out_done, stored = sem("out_done"), sem("stored")
        unfit_done, unfit_ps, flag_done = sem("unfit_done"), sem("unfit_ps"), sem("flag_done")
        g_node_in, g_start, g_iota = sem("g_node_in"), sem("g_start"), sem("g_iota")
        g_freed, g_padded = sem("g_freed"), sem("g_padded")
        g_src, g_dst, g_e, g_src_seen = sem("g_src"), sem("g_dst"), sem("g_e"), sem("g_src_seen")
        g_got = [sem(f"g_got{g}") for g in range(2)]
        g_eT_ps, g_eT_sb, g_H_ps, g_pre, g_rows = (sem(n) for n in ("g_eT_ps", "g_eT_sb", "g_H_ps", "g_pre", "g_rows"))
        g_dst_sb, g_onehot, g_prod = sem("g_dst_sb"), sem("g_onehot"), sem("g_prod")
        g_aggT_ps, g_aggT_sb, g_z_ps, g_z_sb = (sem(n) for n in ("g_aggT_ps", "g_aggT_sb", "g_z_ps", "g_z_sb"))
        g_deg, g_sqrt, g_u, g_stored = (sem(n) for n in ("g_deg", "g_sqrt", "g_u", "g_stored"))

        x_blocks = x[0:(NB - 1) * P, :].rearrange("(b p) f -> p b f", p=P)
        out_blocks = out[0:(NB - 1) * P, :].rearrange("(b p) f -> p b f", p=P)
        x3 = x_s.rearrange("p (b f) -> p b f", f=F)
        rows3 = lambda t: t.rearrange("p (b c) -> p b c", c=GE)
        e_halves = edge[0:NFULL * GE, :].rearrange("(j k p g) f -> j p k g f", k=HALF, p=P, g=2)
        nh = NFULL // HALF

        last_edges = slice(NFULL * GE, E)
        pairs = TAIL // 2
        STEP = NG + 1

        def if_unfit(eng):
            eng.wait_ge(flag_done, 1)
            is_unfit = eng.alloc_register("is_unfit")
            eng.load(is_unfit, flag[0:1, 0:1])
            return eng.If_ne(is_unfit, 0)

        block = ctx.enter_context(nc.Block())

        @block.sync
        def _(sp):
            sp.wait_ge(padded, 1)
            sp.dma_start(x3[:, 0:NB - 1, :], x_blocks).then_inc(x_in, 16)
            sp.dma_start(x3[0:NLAST, NB - 1, :], x[(NB - 1) * P:N, :]).then_inc(x_in, 16)
            sp.wait_ge(filled, 1)
            for dst_ap, src_ap in (
                    (W1n[0:F, 0:F], W1[0:F, :]), (W1n[0:F, F:], W3[0:F, :]),
                    (W1n[F:F + 1, 0:F], b1.unsqueeze(0)), (W1n[F:F + 1, F:], b3.unsqueeze(0)),
                    (W1e[0:F, 0:F], W1[F:, :]), (W1e[F:, F:], W1[F:, :]),
                    (W2b[0:F, :], W2[:, :]), (W2b[F:F + 1, :], b2.unsqueeze(0)),
                    (W3a[:, :], W3[F:, :])):
                sp.dma_start(dst_ap, src_ap).then_inc(w_in, 16)
            def load_half(j, half):
                sp.dma_start(e_ring[:, HALF * half:HALF * half + HALF, :, :],
                             e_halves[j]).then_inc(e_in[half], 16)
            load_half(0, 0)
            load_half(1, 1)
            sp.wait_ge(nodes_sb, 1)
            P3 = Pn_s.rearrange("p (b f) -> p b f", f=F)
            sp.dma_start(P_dram.rearrange("(b p) f -> p b f", p=P), P3).then_inc(P_out, 16)
            sp.dma_start(y3_dram.rearrange("(b p) f -> p b f", p=P), y3[:]).then_inc(y3_out, 16)
            with sp.Fori(1, nh // 2) as c:
                for half in range(2):
                    sp.wait_ge(eT_ps, c * BODY + (half * HALF + HALF - BODY))
                    load_half(c * 2 + half, half)
            sp.wait_ge(padded, 2)
            last = edge[last_edges, :]
            sp.dma_start(e_ring[0:pairs, 0, :, :],
                         last[0:2 * pairs, :].rearrange("(p g) f -> p g f", g=2)).then_inc(e_in[0], 16)
            sp.dma_start(e_ring[pairs:pairs + 1, 0, 0, :], last[2 * pairs:TAIL, :]).then_inc(e_in[0], 16)
            sp.wait_ge(G_added, NG)
            sp.wait_ge(padded, 3)
            sp.dma_start(x_r[:, 0:NB - 1, :], x_blocks).then_inc(xr_in, 16)
            sp.dma_start(x_r[0:NLAST, NB - 1, :], x[(NB - 1) * P:N, :]).then_inc(xr_in, 16)
            sp.wait_ge(out_done, 1)
            sp.dma_start(out_blocks, acc[:, 0:NB - 1, :]).then_inc(stored, 16)
            sp.dma_start(out[(NB - 1) * P:N, :], acc[0:NLAST, NB - 1, :]).then_inc(stored, 16)
            sp.wait_ge(stored, 32)
            with if_unfit(sp):
                sp.wait_ge(g_start, 1)
                sp.wait_ge(y3_out, 16)
                sp.dma_start(y3_g, y3_dram.rearrange("(b p) f -> p b f", p=P)).then_inc(g_node_in, 16)
                sp.dma_start(x2_g[:, 0:NB - 1, :], x_blocks).then_inc(g_node_in, 16)
                sp.dma_start(x2_g[0:NLAST, NB - 1, :], x[(NB - 1) * P:N, :]).then_inc(g_node_in, 16)
                for n in range(4):
                    with sp.Fori(0, NFULL) as k:
                        sp.wait_ge(g_freed, k + (n * NG + 1))
                        ks = bass.ds(k * GE, GE)
                        sp.dma_start(src_g, src[ks].rearrange("(p g) -> p g", g=2)).then_inc(g_src, 16)
                        sp.dma_start(dst_g, dst[ks].rearrange("(p g) -> p g", g=2)).then_inc(g_dst, 16)
                        if n == 0:
                            sp.dma_start(e_g, edge[ks, :].rearrange("(p g) f -> p g f", g=2)).then_inc(g_e, 16)
                    sp.wait_ge(g_padded, n + 1)
                    for flat, tile, landed in ((src, src_g, g_src), (dst, dst_g, g_dst)):
                        sp.dma_start(tile[0:pairs, :], flat[NFULL * GE:NFULL * GE + 2 * pairs].rearrange(
                            "(p g) -> p g", g=2)).then_inc(landed, 16)
                        sp.dma_start(tile[pairs:pairs + 1, 0:1], flat[E - 1:E].unsqueeze(0)).then_inc(landed, 16)
                    if n == 0:
                        sp.dma_start(e_g[0:pairs, :, :],
                                     last[0:2 * pairs, :].rearrange("(p g) f -> p g f", g=2)).then_inc(g_e, 16)
                        sp.dma_start(e_g[pairs:pairs + 1, 0, :], last[2 * pairs:TAIL, :]).then_inc(g_e, 16)
                    sp.wait_ge(g_u, n + 1)
                    if n < 3:
                        sp.dma_start(U_dram.rearrange("(b p) f -> p b f", p=P), u_g).then_inc(g_stored, 16)
                    else:
                        sp.dma_start(out_blocks, acc_g[:, 0:NB - 1, :]).then_inc(g_stored, 16)
                        sp.dma_start(out[(NB - 1) * P:N, :], acc_g[0:NLAST, NB - 1, :]).then_inc(g_stored, 16)
                sp.wait_ge(g_stored, 16 * 5)

        @block.gpsimd
        def _(pool):
            nc.gpsimd.memset(ident[:], 0.0).then_inc(consts, 1)
            pool.wait_ge(consts, 1)
            nc.gpsimd.affine_select(out=ident[:], in_=ident[:], compare_op=ALU.not_equal, fill=1.0,
                                    base=0, pattern=[[-1, P]], channel_multiplier=1).then_inc(consts, 1)
            nc.gpsimd.iota(iota_key[:], [[1, KEYS]], base=0, channel_multiplier=0,
                           allow_small_or_imprecise_dtypes=True)
            nc.gpsimd.iota(iota_r[:], [[1, P]], base=0, channel_multiplier=0,
                           allow_small_or_imprecise_dtypes=True)
            nc.gpsimd.iota(iota_w[:], [[1, W]], base=0, channel_multiplier=0,
                           allow_small_or_imprecise_dtypes=True).then_inc(consts, 1)
            nc.gpsimd.memset(A[:, 0:ZEROED_EARLY, :].bitcast(F32), 0.0).then_inc(cleared0, 1)

            def copy_gidx(k, half):
                nc.gpsimd.tensor_copy(gidx[:, half, :, :], srcT[:, bass.ds(k, HALF), :]).then_inc(gidx_done, 1)

            def gather(slot, g):
                nc.gpsimd.indirect_dma_start(
                    g_ring[:, slot, g, :], None, P_dram[:, :],
                    bass.IndirectOffsetOnAxis(ap=gidx[:, slot // HALF, slot % HALF, g:g + 1], axis=0)
                ).then_inc(gathered[slot], 16)

            def gather_half(c, half, first):
                if not first:
                    pool.wait_ge(pre_done, c * BODY + (half * HALF + HALF - BODY))
                copy_gidx(c * BODY + half * HALF, half)
                pool.wait_ge(gidx_done, c * 2 + (half + 1))
                pool.sem_inc(gidx_seen, 1)
                for kk in range(HALF):
                    for g in range(2):
                        gather(half * HALF + kk, g)

            pool.wait_ge(turned_sb, 8)
            pool.wait_ge(P_out, 16)
            gather_half(0, 0, True)
            gather_half(0, 1, True)
            with pool.Fori(1, NFULL // BODY) as c:
                for half in range(2):
                    gather_half(c, half, False)
            c = NFULL // BODY
            pool.wait_ge(pre_done, NFULL - BODY + HALF)
            nc.gpsimd.tensor_copy(gidx[:, 0, 0, :], srcT[:, NFULL, :]).then_inc(gidx_done, 1)
            pool.wait_ge(gidx_done, 2 * c + 1)
            for g in range(2):
                gather(0, g)

            def fetch(n, k, last_one):
                pool.wait_ge(g_src, 16 * STEP * (n + 1) if last_one else k * 16 + 16 * (STEP * n + 1))
                pool.sem_inc(g_src_seen, 1)
                for g in range(2):
                    nc.gpsimd.indirect_dma_start(
                        got_g[:, g, :], None, (P_dram if n == 0 else U_dram)[:, :],
                        bass.IndirectOffsetOnAxis(ap=src_g[:, g:g + 1], axis=0)).then_inc(g_got[g], 16)

            with if_unfit(pool):
                pool.wait_ge(g_start, 1)
                nc.gpsimd.iota(iota_g, [[1, NPAD]], base=0, channel_multiplier=0,
                               allow_small_or_imprecise_dtypes=True).then_inc(g_iota, 1)
                for n in range(4):
                    if n:
                        pool.wait_ge(g_stored, 16 * n)
                    with pool.Fori(0, NFULL) as k:
                        fetch(n, k, False)
                    fetch(n, NFULL, True)

        @block.scalar
        def _(act):
            act.wait_ge(padded, 1)
            for flat, tile in ((src, src_s), (dst, dst_s)):
                t3 = rows3(tile)
                act.dma_start(t3[:, 0:RB - 1, :],
                              flat[0:(RB - 1) * P * GE].rearrange("(b p c) -> p b c", p=P, c=GE)).then_inc(idx_in, 16)
                act.dma_start(t3[0:RLAST, RB - 1, :],
                              flat[(RB - 1) * P * GE:NFULL * GE].rearrange("(p c) -> p c", c=GE)).then_inc(idx_in, 16)
                act.dma_start(t3[RLAST:RLAST + 1, RB - 1, 0:TAIL],
                              flat[NFULL * GE:E].unsqueeze(0)).then_inc(idx_in, 16)
            act.wait_ge(ln_var, 1)
            nc.scalar.activation(std, var, ACT.Sqrt, bias=epst[:, 0:1], scale=1.0 / F).then_inc(ln_std, 1)
            for t in range(-(-NB // 4)):
                act.wait_ge(hT_ps, t + 1)
                n = min(4, NB - 4 * t) * P
                nc.scalar.copy(hT[0:F, 512 * t:512 * t + n], ps[t % 4][0:F, 0:n]).then_inc(hT_sb, 1)
            for i in range(8):
                act.wait_ge(turned, i + 1)
                kind, g = i // 2, i % 2
                tile = (srcT, keyT, rT, dlT)[kind]
                nc.scalar.copy(tile[:, :, g], ps[i][:, 0:NG]).then_inc(turned_sb, 1)

            def group(k, par, first):
                act.wait_ge(eT_ps, k + 1)
                if not first:
                    act.wait_ge(H_ps, k - 1)
                nc.scalar.copy(eT[:, par, :], ps_eT[par][:, 0:P]).then_inc(eT_sb, 1)
                act.wait_ge(pre_done, k + 1)
                if not first:
                    act.wait_ge(G_ps, k - 1)
                nc.scalar.activation(hid[:, par, :, 0:F], pre[:, par, :, :], ACT.Relu).then_inc(hid_done, 1)

            for k in range(BODY):
                group(k, k % 2, k < 2)
            with act.Fori(1, NFULL // BODY) as c:
                for k in range(BODY):
                    group(c * BODY + k, k % 2, False)
            group(NFULL, 0, False)
            act.wait_ge(ln_var, 2)
            nc.scalar.activation(std, var, ACT.Sqrt, bias=epst[:, 0:1], scale=1.0 / F).then_inc(ln_std, 1)
            act.wait_ge(deg_done, 1)
            nc.scalar.activation(dis, dis, ACT.Sqrt).then_inc(sqrt_done, 1)

            def hidden_rows(k):
                act.wait_ge(g_eT_ps, k + 1)
                nc.scalar.copy(eT_g, ps[5][:, 0:P]).then_inc(g_eT_sb, 1)
                act.wait_ge(g_pre, k + 1)
                nc.scalar.activation(rows_g[:, :, 0:F], pre_g, ACT.Relu).then_inc(g_rows, 1)

            with if_unfit(act):
                with act.Fori(0, NFULL) as k:
                    hidden_rows(k)
                hidden_rows(NFULL)
                act.wait_ge(ln_var, 3)
                nc.scalar.activation(std, var, ACT.Sqrt, bias=epst[:, 0:1], scale=1.0 / F).then_inc(ln_std, 1)
                act.wait_ge(g_deg, 1)
                nc.scalar.activation(dis, dis, ACT.Sqrt).then_inc(g_sqrt, 1)

        @block.tensor
        def _(pe):
            pe.wait_ge(consts, 2)
            pe.wait_ge(w_in, 16 * 9)
            pe.transpose(ps[7][0:F, 0:F + 1], W2b[:, :], ident[0:F + 1, 0:F + 1]).then_inc(wfold_ps, 1)
            pe.wait_ge(wfold_sb, 1)
            pe.matmul(ps[7][0:F + 1, 128:128 + F], W2T[:, :], W3a[:, :], start=True, stop=True).then_inc(wfold_ps, 1)
            pe.wait_ge(h_done, 1)
            for t in range(-(-NB // 4)):
                if t >= 4:
                    pe.wait_ge(hT_sb, t - 3)
                for j in range(4 * t, min(4 * t + 4, NB)):
                    ins = pe.transpose(ps[t % 4][0:F, (j % 4) * P:(j % 4) * P + P],
                                       h_s[:, j * F:j * F + F], ident[:, :])
                ins.then_inc(hT_ps, 1)
            for t in range(-(-NB // 4)):
                pe.wait_ge(hT_sb, t + 1)
                if t >= 3:
                    pe.wait_ge(nodes_ps_read, t - 2)
                for j in range(4 * t, min(4 * t + 4, NB)):
                    ins = pe.matmul(ps[4 + t % 3][:, (j % 4) * P:(j % 4) * P + P],
                                    hT[0:F + 1, j * P:j * P + P], W1n[:, :], start=True, stop=True)
                ins.then_inc(nodes_ps, 1)
            pe.wait_ge(nodes_ps_read, -(-NB // 4))
            pe.wait_ge(hT_sb, -(-NB // 4))
            pe.wait_ge(wfold_sb, 2)
            pe.wait_ge(nat_done, 1)
            for i in range(8):
                kind, g = i // 2, i % 2
                tile = (srcf_s, key_s, rf_s, dl_s)[kind]
                t4 = tile.rearrange("p (b c g) -> p b c g", g=2, c=P)
                for b in range(RB):
                    ins = pe.transpose(ps[i][:, b * P:b * P + P], t4[:, b, :, g], ident[:, :])
                ins.then_inc(turned, 1)
            pe.wait_ge(turned_sb, 1)
            for b in range(RB):
                ins = pe.transpose(ps[0][0:1, b * P:b * P + P], base_n[:, b:b + 1], ident[:, :])
            ins.then_inc(turned, 1)
            pe.wait_ge(base_read, 1)
            pe.wait_ge(turned_sb, 8)

            def turn(k, par, slot, first):
                if not first:
                    pe.wait_ge(eT_sb, k - 1)
                pe.transpose(ps_eT[par][:, 0:P], e_ring[:, slot, :, :].rearrange("p g f -> p (g f)"),
                             ident[:, :]).then_inc(eT_ps, 1)

            def edges(k, par, first):
                pe.wait_ge(eT_sb, k + 1)
                if not first:
                    pe.wait_ge(pre_done, k - 1)
                pe.matmul(ps_H[par][:, 0:P], eT[:, par, :], W1e[:, :], start=True, stop=True).then_inc(H_ps, 1)
                pe.wait_ge(onehots, k + 1)
                if not first:
                    pe.wait_ge(A_added, k - 1)
                for g in range(2):
                    ins = pe.matmul(ps_A[par][:, 0:KEYS], oh_r[:, par, g, :], oh_key[:, par, g, :],
                                    start=(g == 0), stop=(g == 1))
                ins.then_inc(A_ps, 1)

            def sums(k, par, first):
                pe.wait_ge(hid_done, k + 1)
                if not first:
                    pe.wait_ge(G_added, k - 1)
                for g in range(2):
                    ins = pe.matmul(ps_G[par][0:F + 1, 0:W], hid[:, par, g, :], oh_w[:, par, g, :],
                                    start=(g == 0), stop=(g == 1))
                ins.then_inc(G_ps, 1)

            def body(c, first):
                base = c * BODY
                for k in range(BODY):
                    if k % HALF == 0:
                        pe.wait_ge(e_in[k // HALF], c * 16 + 16)
                    turn(base + k, k % 2, k, first and k < 2)
                    if not (first and k == 0):
                        sums(base + (k - 1), (k + 1) % 2, first and k < 3)
                    edges(base + k, k % 2, first and k < 2)

            body(0, True)
            with pe.Fori(1, NFULL // BODY) as c:
                body(c, False)
            pe.wait_ge(e_in[0], 16 * (nh // 2 + 2))
            turn(NFULL, 0, 0, False)
            sums(NFULL - 1, 1, False)
            edges(NFULL, 0, False)
            sums(NFULL, 0, False)
            pe.wait_ge(G_added, NG)
            pe.wait_ge(A_added, NG)
            for t in range(NB // DST_BODY):
                for j in range(DST_BODY):
                    b = t * DST_BODY + j
                    ins = pe.matmul(ps[t][:, j * (F + 1):(j + 1) * (F + 1)], aggT[:, b * P:b * P + P],
                                    W23[:, :], start=True, stop=True)
                ins.then_inc(z_ps, 1)
            pe.wait_ge(unfit_done, 1)
            pe.matmul(ps[5][0:1, 0:1], unfit[:, 0:1], ones[:, :], start=True, stop=True).then_inc(unfit_ps, 1)
            for layer in range(3):
                pe.wait_ge(U_done, layer + 1)
                with pe.Fori(0, NB // DST_BODY) as t:
                    for j in range(DST_BODY):
                        pe.wait_ge(V_read, t * DST_BODY + (layer * NB + j + 1))
                        for q in range(NB):
                            ins = pe.matmul(ps[j][:, 0:3 * F],
                                            A[:, q, bass.ds(t * (DST_BODY * P) + j * P, P)],
                                            U[:, layer % 2, q, :, :].rearrange("p s f -> p (s f)"),
                                            start=(q == 0), stop=(q == NB - 1))
                        ins.then_inc(V_ps, 1)

            def scatter(n, k, last_one):
                if n == 0:
                    pe.wait_ge(g_e, 16 * STEP if last_one else k * 16 + 16)
                    pe.transpose(ps[5][:, 0:P], e_g.rearrange("p g f -> p (g f)"), ident[:, :]).then_inc(g_eT_ps, 1)
                    pe.wait_ge(g_eT_sb, k + 1)
                    pe.matmul(ps[6][:, 0:P], eT_g, W1e[:, :], start=True, stop=True).then_inc(g_H_ps, 1)
                    pe.wait_ge(g_rows, k + 1)
                else:
                    for g in range(2):
                        pe.wait_ge(g_got[g], k * 16 + 16 * (NG * n + 1))
                pe.wait_ge(g_onehot, k + (NG * n + 1))
                width = F1 if n == 0 else F
                for b in range(NB):
                    at = b % DST_BODY * F1
                    for g in range(2):
                        ins = pe.matmul(ps[b // DST_BODY][:, at:at + width], oh_g[:, g, b * P:b * P + P],
                                        (rows_g if n == 0 else got_g)[:, g, :], start=(g == 0), stop=(g == 1))
                ins.then_inc(g_prod, 1)

            with if_unfit(pe):
                for n in range(4):
                    with pe.Fori(0, NFULL) as k:
                        scatter(n, k, False)
                    scatter(n, NFULL, True)
                    if n == 0:
                        pe.wait_ge(g_freed, NG + 1)
                        for b in range(NB):
                            pe.transpose(ps[5][0:F1, 0:P], sums_g[:, b, :], ident[:, :]).then_inc(g_aggT_ps, 1)
                            pe.wait_ge(g_aggT_sb, b + 1)
                            pe.matmul(ps[6][:, 0:F1], aggT[:, b * P:b * P + P], W23[:, :],
                                      start=True, stop=True).then_inc(g_z_ps, 1)
                            pe.wait_ge(g_z_sb, b + 1)

        @block.vector
        def _(dve):
            chain = [0]

            def link(ins):
                chain[0] += 1
                ins.then_inc(link_d, 1)
                dve.wait_ge(link_d, chain[0])

            nc.vector.memset(x3[:, NB - 1, :], 0.0)
            nc.vector.memset(rows3(src_s)[:, RB - 1, :], 0)
            nc.vector.memset(rows3(dst_s)[:, RB - 1, :], FAR).then_inc(padded, 1)
            nc.vector.memset(epst[:], EPS)
            nc.vector.memset(W1e[:], 0.0)
            nc.vector.memset(ones[:], 1.0)
            nc.vector.memset(W23[:], 0.0)
            nc.vector.memset(hT[F:F + 1, :], 1.0)
            nc.vector.memset(aggT[:], 0.0)
            link(nc.vector.memset(hid[:], 1.0))
            nc.vector.memset(W23[F:F + 1, F:F + 1], 1.0).then_inc(filled, 1)

            def layernorm(xt, work, sqt, n):
                per_node = lambda s: s.unsqueeze(2).to_broadcast([P, NB, F])
                link(nc.vector.tensor_reduce(mean, xt, AX.X, ALU.add))
                link(nc.vector.tensor_scalar(mean, mean, 1.0 / F, None, ALU.mult))
                link(nc.vector.tensor_tensor(work, xt, per_node(mean), ALU.subtract))
                link(nc.vector.tensor_tensor(sqt, work, work, ALU.mult))
                nc.vector.tensor_reduce(var, sqt, AX.X, ALU.add).then_inc(ln_var, 1)
                dve.wait_ge(ln_std, n)
                link(nc.vector.reciprocal(rstd, std))
                return nc.vector.scalar_tensor_tensor(out=work, in0=work, scalar=0.0, in1=per_node(rstd),
                                                      op0=ALU.max, op1=ALU.mult)

            dve.wait_ge(x_in, 32)
            layernorm(x3, h_s.rearrange("p (b f) -> p b f", f=F),
                      sq_s.rearrange("p (b f) -> p b f", f=F), 1).then_inc(h_done, 1)
            dve.wait_ge(wfold_ps, 1)
            nc.vector.tensor_copy(W2T[:, :], ps[7][0:F, 0:F + 1]).then_inc(wfold_sb, 1)
            dve.wait_ge(wfold_ps, 2)
            nc.vector.tensor_copy(W23[:, 0:F], ps[7][0:F + 1, 128:128 + F]).then_inc(wfold_sb, 1)
            dve.wait_ge(idx_in, 96)
            nc.vector.tensor_copy(srcf_s, src_s)
            nc.vector.tensor_scalar(ri_s, src_s, P - 1, None, ALU.bitwise_and)
            link(nc.vector.tensor_reduce(base_n[:], rows3(dst_s), AX.X, ALU.min))
            link(nc.vector.tensor_copy(rf_s, ri_s))
            nc.vector.tensor_tensor(qr_s, srcf_s, rf_s, ALU.subtract)
            link(nc.vector.tensor_tensor(rows3(key_s), rows3(dst_s),
                                         base_n[:].unsqueeze(2).to_broadcast([P, RB, GE]), ALU.subtract))
            link(nc.vector.tensor_scalar(dl_s, key_s, W - 0.5, NO_SLOT, ALU.is_gt, ALU.mult))
            nc.vector.tensor_reduce(unfit[:, 0:1], dl_s, AX.X, ALU.add)
            link(nc.vector.tensor_tensor(dl_s, dl_s, key_s, ALU.max))
            link(nc.vector.tensor_scalar(dl_s, dl_s, NO_SLOT, None, ALU.min))
            nc.vector.scalar_tensor_tensor(out=key_s, in0=qr_s, scalar=float(W) / P, in1=dl_s,
                                           op0=ALU.mult, op1=ALU.add).then_inc(nat_done, 1)
            P3 = Pn_s.rearrange("p (b f) -> p b f", f=F)
            for t in range(-(-NB // 4)):
                n = min(4, NB - 4 * t)
                dve.wait_ge(nodes_ps, t + 1)
                part = ps[4 + t % 3][:, 0:n * P].rearrange("p (j c) -> p j c", c=P)
                nc.vector.tensor_copy(y3[:, 4 * t:4 * t + n, :], part[:, :, F:])
                ins = nc.vector.tensor_copy(P3[:, 4 * t:4 * t + n, :], part[:, :, 0:F])
                ins.then_inc(nodes_ps_read, 1)
            dve.wait_ge(nodes_ps_read, -(-NB // 4))
            nc.vector.engine_nop().then_inc(nodes_sb, 1)
            dve.wait_ge(turned, 9)
            nc.vector.tensor_copy(base_row[:], ps[0][0:1, :]).then_inc(base_read, 1)
            dve.wait_ge(base_read, 1)
            dve.wait_ge(turned_sb, 8)
            dve.wait_ge(P_out, 16)
            dve.wait_ge(consts, 3)
            dve.wait_ge(cleared0, 1)
            link(nc.vector.memset(A[:, ZEROED_EARLY:, :].bitcast(F32), 0.0))

            def make_onehots(k, par, first):
                if not first:
                    dve.wait_ge(A_ps, k - 1)
                    dve.wait_ge(G_ps, k - 1)
                nc.vector.tensor_tensor(
                    oh_w[:, par, :, :], iota_w[:].unsqueeze(1).to_broadcast([P, 2, W]),
                    dlT[:, bass.ds(k, 1), :].rearrange("p k g -> p (k g)").unsqueeze(2).to_broadcast([P, 2, W]),
                    ALU.is_equal)
                for g in range(2):
                    nc.vector.tensor_scalar(oh_r[:, par, g, :], iota_r[:],
                                            rT[:, bass.ds(k, 1), g], None, ALU.is_equal)
                    ins = nc.vector.tensor_scalar(oh_key[:, par, g, :], iota_key[:],
                                                  keyT[:, bass.ds(k, 1), g], None, ALU.is_equal)
                ins.then_inc(onehots, 1)

            def add_gathered(c, k, par, slot, first):
                dve.wait_ge(gathered[slot], c * 32 + 32)
                dve.wait_ge(H_ps, k + 1)
                if not first:
                    dve.wait_ge(hid_done, k - 1)
                nc.vector.tensor_tensor(pre[:, par, :, :],
                                        ps_H[par][:, 0:P].rearrange("p (g f) -> p g f", g=2),
                                        g_ring[:, slot, :, :], ALU.add).then_inc(pre_done, 1)

            def add_windows(k, par, base, first):
                dve.wait_ge(A_ps, k + 1)
                if not first:
                    dve.wait_ge(A_added, k)
                Aw = A[:, :, bass.ds(base, W)]
                nc.vector.tensor_tensor(Aw, Aw, ps_A[par][:, 0:KEYS].rearrange("p (q w) -> p q w", w=W),
                                        ALU.add).then_inc(A_added, 1)
                dve.wait_ge(G_ps, k + 1)
                if not first:
                    dve.wait_ge(G_added, k)
                Gw = aggT[:, bass.ds(base, W)]
                nc.vector.tensor_tensor(Gw, Gw, ps_G[par][0:F + 1, 0:W], ALU.add).then_inc(G_added, 1)

            def load_base(k, n):
                _, vals = nc.values_load_multi_w_load_instructions(
                    base_row[0:1, bass.ds(k, n)], engines=[mybir.EngineType.DVE], min_val=0, max_val=NPAD - W,
                    skip_runtime_bounds_check_because="a destination is below N, and N + W is below the padded width")
                return vals

            def body(c, first):
                k0 = c * BODY
                if first:
                    vals = load_base(0, BODY)
                else:
                    vals = load_base(k0 - 1, BODY + 1)
                for k in range(BODY):
                    make_onehots(k0 + k, k % 2, first and k < 2)
                    if not (first and k == 0):
                        add_windows(k0 + (k - 1), (k + 1) % 2, vals[k - 1 if first else k], first and k == 1)
                    add_gathered(c, k0 + k, k % 2, k, first and k < 2)

            body(0, True)
            with dve.Fori(1, NFULL // BODY) as c:
                body(c, False)
            vals = load_base(NFULL - 1, 2)
            dve.wait_ge(eT_ps, NFULL - BODY + 1)
            nc.vector.memset(e_ring[:, 0, :, :], 0.0).then_inc(padded, 1)
            make_onehots(NFULL, 0, False)
            add_windows(NFULL - 1, 1, vals[0], False)
            add_gathered(NFULL // BODY, NFULL, 0, 0, False)
            add_windows(NFULL, 0, vals[1], False)
            dve.wait_ge(G_ps, NG)
            dve.wait_ge(G_added, NG)
            nc.vector.memset(x_r[:, NB - 1, :], 0.0).then_inc(padded, 1)
            for t in range(NB // DST_BODY):
                dve.wait_ge(z_ps, t + 1)
                z = ps[t][:, 0:DST_BODY * (F + 1)].rearrange("p (j c) -> p j c", c=F + 1)
                s = slice(t * DST_BODY, (t + 1) * DST_BODY)
                nc.vector.tensor_copy(deg[:, s], z[:, :, F])
                nc.vector.tensor_tensor(y3[:, s, :], y3[:, s, :], z[:, :, 0:F], ALU.add).then_inc(V_read, 1)
            dve.wait_ge(V_read, DST_BODY)
            nc.vector.tensor_scalar(dis, deg, 1.0, None, ALU.max).then_inc(deg_done, 1)
            dve.wait_ge(xr_in, 32)
            link(nc.vector.scalar_tensor_tensor(out=y3[:], in0=y3[:], scalar=0.0, in1=x_r, op0=ALU.max, op1=ALU.add))
            link(layernorm(y3[:], acc[:], sq_r, 2))
            dve.wait_ge(sqrt_done, 1)
            link(nc.vector.reciprocal(dis, dis))
            link(nc.vector.scalar_tensor_tensor(out=dis, in0=deg, scalar=0.5, in1=dis, op0=ALU.is_gt, op1=ALU.mult))

            def split(which, s, value):
                for part in range(2):
                    link(nc.vector.tensor_copy(U[:, which, s, part, :], value))
                    link(nc.vector.tensor_tensor(value, value, U[:, which, s, part, :], ALU.subtract))
                return nc.vector.tensor_copy(U[:, which, s, 2, :], value)

            for t in range(NB // DST_BODY):
                s = slice(t * DST_BODY, (t + 1) * DST_BODY)
                d = dis[:, s].unsqueeze(2).to_broadcast([P, DST_BODY, F])
                link(nc.vector.tensor_tensor(u[:], acc[:, s, :], d, ALU.mult))
                ins = split(0, s, u[:])
                link(ins)
            nc.vector.engine_nop().then_inc(U_done, 1)
            link(nc.vector.tensor_scalar(mean, deg, MAX_EXACT + 0.5, NO_SLOT, ALU.is_gt, ALU.mult))
            link(nc.vector.tensor_reduce(unfit[:, 1:2], mean, AX.X, ALU.add))
            nc.vector.tensor_tensor(unfit[:, 0:1], unfit[:, 0:1], unfit[:, 1:2], ALU.add).then_inc(unfit_done, 1)
            dve.wait_ge(unfit_ps, 1)
            nc.vector.tensor_scalar(flag[:], ps[5][0:1, 0:1], NO_SLOT * (GE - TAIL + 0.5), None,
                                    ALU.is_gt).then_inc(flag_done, 1)
            for layer in range(3):
                for b in range(NB):
                    j = b % DST_BODY
                    d = dis[:, b:b + 1]
                    dve.wait_ge(V_ps, layer * NB + b + 1)
                    V3 = ps[j][:, 0:3 * F].rearrange("p (s f) -> p f s", f=F)
                    nc.vector.tensor_reduce(v[:, j, :], V3, AX.X, ALU.add).then_inc(V_read, 1)
                    dve.wait_ge(V_read, layer * NB + b + 1 + DST_BODY)
                    link(nc.vector.tensor_scalar(v[:, j, :], v[:, j, :], d, None, ALU.mult))
                    link(nc.vector.tensor_tensor(acc[:, b, :], acc[:, b, :], v[:, j, :], ALU.add))
                    if layer < 2:
                        link(nc.vector.tensor_scalar(u[:, j, :], v[:, j, :], d, None, ALU.mult))
                        link(split((layer + 1) % 2, b, u[:, j, :]))
                if layer < 2:
                    nc.vector.engine_nop().then_inc(U_done, 1)
            nc.vector.scalar_tensor_tensor(out=acc[:], in0=acc[:], scalar=0.25, in1=y3[:],
                                           op0=ALU.mult, op1=ALU.add).then_inc(out_done, 1)

            def general():
                link(nc.vector.memset(rows_g, 1.0))
                link(nc.vector.memset(x2_g[:, NB - 1, :], 0.0))
                link(nc.vector.memset(sums_g, 0.0))
                nc.vector.engine_nop().then_inc(g_start, 1)
                nc.vector.engine_nop().then_inc(g_freed, 1)
                dve.wait_ge(g_iota, 1)

                def onehot_and_sum(n, k, last_one):
                    dve.wait_ge(g_dst, 16 * STEP * (n + 1) if last_one else k * 16 + 16 * (STEP * n + 1))
                    nc.vector.tensor_copy(dstf_g, dst_g).then_inc(g_dst_sb, 1)
                    dve.wait_ge(g_dst_sb, k + (n * NG + 1))
                    for g in range(2):
                        ins = nc.vector.tensor_scalar(oh_g[:, g, :], iota_g, dstf_g[:, g:g + 1], None, ALU.is_equal)
                    ins.then_inc(g_onehot, 1)
                    if n == 0:
                        dve.wait_ge(g_H_ps, k + 1)
                        for g in range(2):
                            dve.wait_ge(g_got[g], k * 16 + 16)
                        nc.vector.tensor_tensor(pre_g, ps[6][:, 0:P].rearrange("p (g f) -> p g f", g=2),
                                                got_g, ALU.add).then_inc(g_pre, 1)
                    width = F1 if n == 0 else F
                    dve.wait_ge(g_prod, k + (n * NG + 1))
                    for t in range(NB // DST_BODY):
                        part = ps[t][:, 0:DST_BODY * F1].rearrange("p (j c) -> p j c", c=F1)[:, :, 0:width]
                        into = sums_g[:, t * DST_BODY:(t + 1) * DST_BODY, 0:width]
                        ins = nc.vector.tensor_tensor(into, into, part, ALU.add)
                    ins.then_inc(g_freed, 1)
                    dve.wait_ge(g_freed, k + (n * NG + 2))

                per_node = lambda t: t.unsqueeze(2).to_broadcast([P, NB, F])
                for n in range(4):
                    with dve.Fori(0, NFULL) as k:
                        onehot_and_sum(n, k, False)
                    nc.vector.memset(src_g, 0)
                    nc.vector.memset(e_g, 0.0)
                    nc.vector.memset(dst_g, FAR).then_inc(g_padded, 1)
                    onehot_and_sum(n, NFULL, True)
                    if n == 0:
                        dve.wait_ge(g_node_in, 48)
                        for b in range(NB):
                            dve.wait_ge(g_aggT_ps, b + 1)
                            nc.vector.tensor_copy(aggT[:, b * P:b * P + P], ps[5][0:F1, 0:P]).then_inc(g_aggT_sb, 1)
                            dve.wait_ge(g_z_ps, b + 1)
                            nc.vector.tensor_copy(deg[:, b:b + 1], ps[6][:, F:F1])
                            nc.vector.tensor_tensor(y3_g[:, b, :], y3_g[:, b, :], ps[6][:, 0:F],
                                                    ALU.add).then_inc(g_z_sb, 1)
                        dve.wait_ge(g_z_sb, NB)
                        nc.vector.tensor_scalar(dis, deg, 1.0, None, ALU.max).then_inc(g_deg, 1)
                        link(nc.vector.scalar_tensor_tensor(out=x2_g, in0=y3_g, scalar=0.0, in1=x2_g,
                                                            op0=ALU.max, op1=ALU.add))
                        link(layernorm(x2_g, acc_g, sq_g, 3))
                        dve.wait_ge(g_sqrt, 1)
                        link(nc.vector.reciprocal(dis, dis))
                        link(nc.vector.scalar_tensor_tensor(out=dis, in0=deg, scalar=0.5, in1=dis,
                                                            op0=ALU.is_gt, op1=ALU.mult))
                        nc.vector.tensor_tensor(u_g, acc_g, per_node(dis), ALU.mult).then_inc(g_u, 1)
                    else:
                        link(nc.vector.tensor_tensor(sq_g, sums_g[:, :, 0:F], per_node(dis), ALU.mult))
                        link(nc.vector.tensor_tensor(acc_g, acc_g, sq_g, ALU.add))
                        if n < 3:
                            dve.wait_ge(g_stored, 16 * n)
                            nc.vector.tensor_tensor(u_g, sq_g, per_node(dis), ALU.mult).then_inc(g_u, 1)
                        else:
                            nc.vector.scalar_tensor_tensor(out=acc_g, in0=acc_g, scalar=0.25, in1=x2_g,
                                                           op0=ALU.mult, op1=ALU.add).then_inc(g_u, 1)
                    if n < 3:
                        link(nc.vector.memset(sums_g, 0.0))

            with if_unfit(dve):
                general()


_INS = ['x', 'src', 'dst', 'edge_attr_64', 'L0_gnn_W1', 'L0_gnn_b1', 'L0_gnn_W2', 'L0_gnn_b2', 'L0_gnn_W3', 'L0_gnn_b3']


def kernel(**inputs):
    import numpy as _np
    import concourse.bacc as _bacc
    from concourse import mybir as _mybir
    from concourse.bass_utils import run_bass_kernel_spmd as _run

    nc = _bacc.Bacc("TRN2", target_bir_lowering=False, num_devices=1)
    arrays, args = {}, []
    for name in _INS:
        a = _np.ascontiguousarray(inputs[name])
        arrays[f"in_{name}_dram"] = a
        args.append(nc.dram_tensor(f"in_{name}_dram", a.shape, _mybir.dt.from_np(a.dtype), kind="ExternalInput").ap())
    args.append(nc.dram_tensor("out_0_dram", inputs['x'].shape, F32, kind="ExternalOutput").ap())
    gnn_and_propagation(nc, *args)
    r = _run(nc, [arrays], core_ids=[0])
    return r.results[0]["out_0_dram"]
```

```python
from contextlib import ExitStack

import concourse.bass as bass
from concourse import mybir

ALU = mybir.AluOpType
ACT = mybir.ActivationFunctionType
AX = mybir.AxisListType
F32 = mybir.dt.float32
F16 = mybir.dt.float16
BF16 = mybir.dt.bfloat16
I32 = mybir.dt.int32

P = 128
F = 64
W = 12
HALF = 3
BODY = 2 * HALF
MAX_EXACT = 256
FAR = 1 << 20
NO_SLOT = 1000.0
EPS = 1e-5
PIECE = 5
QUAD = 4
LAYERS = 3
SPLIT_STEPS = 4


def gnn_and_propagation(nc, x, src, dst, edge, W1, b1, W2, b2, W3, b3, out):
    N, E = x.shape[0], src.shape[0]
    NB = -(-N // P)
    NPAD = NB * P
    NLAST = N - (NB - 1) * P
    GE = 2 * P
    NG = -(-E // GE)
    NFULL = E // GE
    TAIL = E - NFULL * GE
    NBODY = NFULL // BODY
    RB = -(-NG // P)
    RLAST = NFULL - (RB - 1) * P
    KEYS = NB * W
    QUADS = -(-NB // QUAD)
    F1 = F + 1
    assert NFULL % BODY == 0 and NG == NFULL + 1 and TAIL > P and TAIL % 2 == 1 and NB % PIECE == 0
    assert N - 1 + W <= NPAD and KEYS <= 512 and NFULL + BODY <= RB * P

    with ExitStack() as ctx:
        def sb(name, shape, dt, stack=ctx):
            return stack.enter_context(nc.sbuf_tensor(name, shape, dt))

        def sem(name):
            return ctx.enter_context(nc.semaphore(name))

        P_dram = nc.dram_tensor("node_part", (NPAD, F), F32).ap()
        y3_dram = nc.dram_tensor("node_update", (NPAD, F), F32).ap()
        U_dram = nc.dram_tensor("scaled", (NPAD, F), F32).ap()

        A = sb("A", [P, NB, NPAD], BF16)

        def slab(q, n=1, dt=F32):
            return A[:, q:q + n, :].rearrange("p a b -> p (a b)").bitcast(dt)

        NS = RB * GE
        NUMBERS, ROWS = 15, 21

        def numbers(i, dt=F32):
            return slab(NUMBERS, 5, dt)[:, i * NS:(i + 1) * NS]

        src_s, dst_s, ri_s = (numbers(i, I32) for i in range(3))
        srcf_s, rf_s, key_s, dl_s = (numbers(i) for i in range(3, 7))
        fold_place = slab(NUMBERS, 5)[:, 7 * NS:7 * NS + 4 * F]
        W2b = fold_place[0:F1, 0:F]
        W3a = fold_place[0:F, F:2 * F]
        W2T = fold_place[0:F, 2 * F:2 * F + F1]
        rows_place = slab(ROWS, 2)
        PAIRS = -(-NB // 2)
        hT = rows_place[:, 0:PAIRS * P]
        after_hT = rows_place[:, PAIRS * P:]
        W1n, W3n = after_hT[:, 0:P], after_hT[:, P:2 * P]
        b1_all = after_hT[:, 2 * P:2 * P + F]
        b3_row = after_hT[0:1, 3 * P:4 * P]
        ones_row = after_hT[0:1, 4 * P:5 * P]
        P_s, h_s = slab(23), slab(24)

        node3 = lambda t: t.rearrange("p (b f) -> p b f", f=F)
        x2_g, acc_g, y3_g, sq_g, u_g = (node3(slab(q)) for q in (0, 1, 2, 12, 13))
        sums_g = slab(3, 2)[:, 0:NB * F1].rearrange("p (b c) -> p b c", c=F1)
        iota_g = slab(5, 2)
        oh_g = slab(7, 4).rearrange("p (g n) -> p g n", g=2)
        small_g = slab(11)
        e_g = small_g[:, 0:2 * F].rearrange("p (g f) -> p g f", g=2)
        got_g = small_g[:, 2 * F:4 * F].rearrange("p (g f) -> p g f", g=2)
        eT_g = small_g[:, 4 * F:6 * F]
        pre_g = small_g[:, 6 * F:8 * F].rearrange("p (g f) -> p g f", g=2)
        rows_g = small_g[:, 8 * F:8 * F + 2 * F1].rearrange("p (g c) -> p g c", g=2)
        dstf_g = small_g[:, 12 * F:12 * F + 2]
        src_g = slab(11, 1, I32)[:, 13 * F:13 * F + 2]
        dst_g = slab(11, 1, I32)[:, 14 * F:14 * F + 2]

        ident = sb("ident", [P, P], F32)
        ones = sb("ones", [P, 1], F32)
        W1e = sb("W1e", [P, P], F32)
        W23 = sb("W23", [F1, F1], F32)
        stat = sb("stat", [P, 8, NB], F32)
        mean, var, std, rstd, deg, dis, dis2, gap = (stat[:, i, :] for i in range(8))
        bn = sb("bn", [P, NB, 6], F32)
        epst = sb("epst", [P, 1], F32)
        unfit = sb("unfit", [P, 2], F32)
        flag = sb("flag", [1, 1], I32)
        base_n = sb("base_n", [P, RB], F32)
        base_row = sb("base_row", [1, RB * P], I32)
        y3 = sb("y3", [P, NB, F], F32)
        aggT = sb("aggT", [F1, NPAD], F32)
        acc = sb("acc", [P, NB, F], F32)

        edge_phase = ExitStack()

        def eb(name, shape, dt):
            return sb(name, shape, dt, edge_phase)

        srcT = eb("srcT", [P, NFULL + BODY, 2], I32)
        keyT = eb("keyT", [P, NG, 2], F16)
        rT = eb("rT", [P, NG, 2], BF16)
        dlT = eb("dlT", [P, NG, 2], BF16)
        iota_key = eb("iota_key", [P, KEYS], F16)
        iota_r = eb("iota_r", [P, P], BF16)
        iota_w = eb("iota_w", [P, W], F32)
        e_ring = eb("e_ring", [P, BODY, 2, F], F32)
        g_ring = eb("g_ring", [P, BODY, 2, F], F32)
        gidx = eb("gidx", [P, BODY, 2], I32)
        eT = eb("eT", [P, 2, P], F32)
        hid = eb("hid", [P, 3, 2, F1], F32)
        oh_key = eb("oh_key", [P, 2, 2, KEYS], BF16)
        oh_r = eb("oh_r", [P, 2, 2, P], BF16)
        oh_w = eb("oh_w", [P, 3, 2, W], F32)
        edge_phase.close()

        prop_phase = ExitStack()

        def pb(name, shape, dt):
            return sb(name, shape, dt, prop_phase)

        U = pb("U", [P, NB, 3, F], BF16)
        U_next = pb("U_next", [P, NB, 3, F], BF16)
        v = pb("v", [P, 2, F], F32)
        rem = pb("rem", [P, 2, F], F32)
        prop_phase.close()
        u_first = U_next[:].rearrange("p b s f -> p (b s f)").bitcast(F32)[:, 0:NB * F].rearrange(
            "p (b f) -> p b f", f=F)

        ps = [ctx.enter_context(nc.psum_tensor(f"ps{i}", [P, 512], F32)) for i in range(8)]
        ps_eT, ps_H, ps_A, ps_G = ps[0:2], ps[2:4], ps[4:6], ps[6:8]

        padded = sem("padded")
        x_in, src_in, dst_in, w_in = sem("x_in"), sem("src_in"), sem("dst_in"), sem("w_in")
        consts = sem("consts")
        cleared = [sem(f"cleared{i}") for i in range(4)]
        filled = sem("filled")
        link_d = sem("link_d")
        ln_var, ln_std = sem("ln_var"), sem("ln_std")
        hn_sub, hn_done = sem("hn_sub"), sem("hn_done")
        hT_ps, hT_sb = sem("hT_ps"), sem("hT_sb")
        nodes_ps, P_sb, y3_ps, y3_sb = sem("nodes_ps"), sem("P_sb"), sem("y3_ps"), sem("y3_sb")
        P_out, y3_out = sem("P_out"), sem("y3_out")
        srcf_done, ri_done, rf_done, nat_done = (sem(n) for n in ("srcf_done", "ri_done", "rf_done", "nat_done"))
        src_turned, srcT_done = sem("src_turned"), sem("srcT_done")
        turned, turned_sb = sem("turned"), sem("turned_sb")
        base_turned, base_read = sem("base_turned"), sem("base_read")
        wfold_ps, wfold_sb = sem("wfold_ps"), sem("wfold_sb")
        e_in = [sem(f"e_in{i}") for i in range(2)]
        gathered = [sem(f"gathered{i}") for i in range(BODY)]
        gidx_done, gidx_seen = sem("gidx_done"), sem("gidx_seen")
        eT_ps, eT_sb = sem("eT_ps"), sem("eT_sb")
        H_ps, hid_done = sem("H_ps"), sem("hid_done")
        onehots = sem("onehots")
        A_ps, A_added = sem("A_ps"), sem("A_added")
        G_ps, G_added = sem("G_ps"), sem("G_added")
        z_ps, x2_sum = sem("z_ps"), sem("x2_sum")
        deg_done, sqrt_done = sem("deg_done"), sem("sqrt_done")
        xc_done, h2_done = sem("xc_done"), sem("h2_done")
        u_done, hi_done, r_done, mid_done = (sem(n) for n in ("u_done", "hi_done", "r_done", "mid_done"))
        U_done = sem("U_done")
        V_ps, V_read = sem("V_ps"), sem("V_read")
        split_done = sem("split_done")
        out_done, stored = sem("out_done"), sem("stored")
        unfit_done, unfit_ps, flag_done = sem("unfit_done"), sem("unfit_ps"), sem("flag_done")
        g_node_in, g_start, g_iota = sem("g_node_in"), sem("g_start"), sem("g_iota")
        g_freed, g_padded = sem("g_freed"), sem("g_padded")
        g_src, g_dst, g_e, g_src_seen = sem("g_src"), sem("g_dst"), sem("g_e"), sem("g_src_seen")
        g_got = [sem(f"g_got{g}") for g in range(2)]
        g_eT_ps, g_eT_sb, g_H_ps, g_pre, g_rows = (sem(n) for n in ("g_eT_ps", "g_eT_sb", "g_H_ps", "g_pre", "g_rows"))
        g_dst_sb, g_onehot, g_prod = sem("g_dst_sb"), sem("g_onehot"), sem("g_prod")
        g_aggT_ps, g_aggT_sb, g_z_ps, g_z_sb = (sem(n) for n in ("g_aggT_ps", "g_aggT_sb", "g_z_ps", "g_z_sb"))
        g_deg, g_sqrt, g_u, g_stored = (sem(n) for n in ("g_deg", "g_sqrt", "g_u", "g_stored"))

        PIECES = NB // PIECE
        LOADS = 12
        x_blocks = x[0:(NB - 1) * P, :].rearrange("(b p) f -> p b f", p=P)
        out_blocks = out[0:(NB - 1) * P, :].rearrange("(b p) f -> p b f", p=P)

        def rows3(t):
            return t.rearrange("p (b c) -> p b c", c=GE)

        def nodes3(t):
            return t.rearrange("p (b f) -> p b f", f=F)

        def quad(t):
            return slice(QUAD * t, min(QUAD * t + QUAD, NB))

        def piece(t):
            return slice(PIECE * t, PIECE * t + PIECE)

        e_halves = edge[0:NFULL * GE, :].rearrange("(j k p g) f -> j p k g f", k=HALF, p=P, g=2)
        last_edges = slice(NFULL * GE, E)
        pairs = TAIL // 2
        STEP = NG + 1

        def if_unfit(eng):
            eng.wait_ge(flag_done, 1)
            is_unfit = eng.alloc_register("is_unfit")
            eng.load(is_unfit, flag[0:1, 0:1])
            return eng.If_ne(is_unfit, 0)

        block = ctx.enter_context(nc.Block())

        @block.sync
        def _(sp):
            sp.wait_ge(padded, 1)
            sp.dma_start(acc[:, 0:NB - 1, :], x_blocks).then_inc(x_in, 16)
            sp.dma_start(acc[0:NLAST, NB - 1, :], x[(NB - 1) * P:N, :]).then_inc(x_in, 16)
            sp.wait_ge(filled, 1)
            for dst_ap, src_ap in (
                    (W1n[0:F, 0:F], W1[0:F, :]), (W1n[F:, F:], W1[0:F, :]),
                    (W3n[0:F, 0:F], W3[0:F, :]), (W3n[F:, F:], W3[0:F, :]),
                    (b1_all, b1.unsqueeze(0).to_broadcast([P, F])), (b3_row[:, 0:F], b3.unsqueeze(0)), (b3_row[:, F:], b3.unsqueeze(0)),
                    (W1e[0:F, 0:F], W1[F:, :]), (W1e[F:, F:], W1[F:, :]),
                    (W2b[0:F, :], W2[:, :]), (W2b[F:F1, :], b2.unsqueeze(0)),
                    (W3a[:, :], W3[F:, :])):
                sp.dma_start(dst_ap, src_ap).then_inc(w_in, 16)

            def load_half(j, half):
                sp.dma_start(e_ring[:, HALF * half:HALF * half + HALF, :, :],
                             e_halves[j]).then_inc(e_in[half], 16)

            P_blocks = P_dram.rearrange("(b p) f -> p b f", p=P)
            for t in range(QUADS):
                sp.wait_ge(P_sb, t + 1)
                sp.dma_start(P_blocks[:, quad(t), :], nodes3(P_s)[:, quad(t), :]).then_inc(P_out, 16)
            load_half(0, 0)
            load_half(1, 1)
            sp.wait_ge(y3_sb, QUADS)
            sp.dma_start(y3_dram.rearrange("(b p) f -> p b f", p=P), y3[:]).then_inc(y3_out, 16)
            with sp.Fori(1, NBODY) as c:
                for half in range(2):
                    sp.wait_ge(eT_ps, c * BODY + (half * HALF + HALF - BODY))
                    load_half(c * 2 + half, half)
            sp.wait_ge(padded, 2)
            last = edge[last_edges, :]
            sp.dma_start(e_ring[0:pairs, 0, :, :],
                         last[0:2 * pairs, :].rearrange("(p g) f -> p g f", g=2)).then_inc(e_in[0], 16)
            sp.dma_start(e_ring[pairs:pairs + 1, 0, 0, :], last[2 * pairs:TAIL, :]).then_inc(e_in[0], 16)
            sp.wait_ge(y3_out, 16)
            for t in range(PIECES):
                sp.wait_ge(out_done, t + 1)
                full = slice(PIECE * t, min(PIECE * t + PIECE, NB - 1))
                sp.dma_start(out_blocks[:, full, :], acc[:, full, :]).then_inc(stored, 16)
            sp.dma_start(out[(NB - 1) * P:N, :], acc[0:NLAST, NB - 1, :]).then_inc(stored, 16)
            sp.wait_ge(stored, 16 * (PIECES + 1))
            with if_unfit(sp):
                sp.wait_ge(g_start, 1)
                sp.dma_start(y3_g, y3_dram.rearrange("(b p) f -> p b f", p=P)).then_inc(g_node_in, 16)
                sp.dma_start(x2_g[:, 0:NB - 1, :], x_blocks).then_inc(g_node_in, 16)
                sp.dma_start(x2_g[0:NLAST, NB - 1, :], x[(NB - 1) * P:N, :]).then_inc(g_node_in, 16)
                for n in range(4):
                    with sp.Fori(0, NFULL) as k:
                        sp.wait_ge(g_freed, k + (n * NG + 1))
                        ks = bass.ds(k * GE, GE)
                        sp.dma_start(src_g, src[ks].rearrange("(p g) -> p g", g=2)).then_inc(g_src, 16)
                        sp.dma_start(dst_g, dst[ks].rearrange("(p g) -> p g", g=2)).then_inc(g_dst, 16)
                        if n == 0:
                            sp.dma_start(e_g, edge[ks, :].rearrange("(p g) f -> p g f", g=2)).then_inc(g_e, 16)
                    sp.wait_ge(g_padded, n + 1)
                    for flat, tile, landed in ((src, src_g, g_src), (dst, dst_g, g_dst)):
                        sp.dma_start(tile[0:pairs, :], flat[NFULL * GE:NFULL * GE + 2 * pairs].rearrange(
                            "(p g) -> p g", g=2)).then_inc(landed, 16)
                        sp.dma_start(tile[pairs:pairs + 1, 0:1], flat[E - 1:E].unsqueeze(0)).then_inc(landed, 16)
                    if n == 0:
                        sp.dma_start(e_g[0:pairs, :, :],
                                     last[0:2 * pairs, :].rearrange("(p g) f -> p g f", g=2)).then_inc(g_e, 16)
                        sp.dma_start(e_g[pairs:pairs + 1, 0, :], last[2 * pairs:TAIL, :]).then_inc(g_e, 16)
                    sp.wait_ge(g_u, n + 1)
                    if n < 3:
                        sp.dma_start(U_dram.rearrange("(b p) f -> p b f", p=P), u_g).then_inc(g_stored, 16)
                    else:
                        sp.dma_start(out_blocks, acc_g[:, 0:NB - 1, :]).then_inc(g_stored, 16)
                        sp.dma_start(out[(NB - 1) * P:N, :], acc_g[0:NLAST, NB - 1, :]).then_inc(g_stored, 16)
                sp.wait_ge(g_stored, 16 * 5)

        @block.gpsimd
        def _(pool):
            nc.gpsimd.memset(ident[:], 0.0).then_inc(consts, 1)
            pool.wait_ge(consts, 1)
            nc.gpsimd.affine_select(out=ident[:], in_=ident[:], compare_op=ALU.not_equal, fill=1.0,
                                    base=0, pattern=[[-1, P]], channel_multiplier=1).then_inc(consts, 1)
            nc.gpsimd.iota(iota_key[:], [[1, KEYS]], base=0, channel_multiplier=0,
                           allow_small_or_imprecise_dtypes=True)
            nc.gpsimd.iota(iota_r[:], [[1, P]], base=0, channel_multiplier=0,
                           allow_small_or_imprecise_dtypes=True)
            nc.gpsimd.iota(iota_w[:], [[1, W]], base=0, channel_multiplier=0,
                           allow_small_or_imprecise_dtypes=True).then_inc(consts, 1)
            nc.gpsimd.memset(A[:, 0:NUMBERS, :].bitcast(F32), 0.0).then_inc(cleared[0], 1)

            def gather(slot):
                for g in range(2):
                    nc.gpsimd.indirect_dma_start(
                        g_ring[:, slot, g, :], None, P_dram[:, :],
                        bass.IndirectOffsetOnAxis(ap=gidx[:, slot, g:g + 1], axis=0)
                    ).then_inc(gathered[slot], 16)

            pool.wait_ge(P_out, 16 * QUADS)
            pool.wait_ge(gidx_done, 1)
            for slot in range(BODY):
                gather(slot)
            pool.wait_ge(turned_sb, 6)
            pool.wait_ge(wfold_sb, 2)
            nc.gpsimd.memset(slab(NUMBERS + 4), 0.0).then_inc(cleared[1], 1)
            with pool.Fori(1, NBODY) as c:
                for slot in range(BODY):
                    pool.wait_ge(gidx_done, c * BODY + (slot + 2 - BODY))
                    pool.sem_inc(gidx_seen, 1)
                    gather(slot)
            pool.wait_ge(gidx_done, NFULL + 2 - BODY)
            gather(0)

            def fetch(n, k, last_one):
                pool.wait_ge(g_src, 16 * STEP * (n + 1) if last_one else k * 16 + 16 * (STEP * n + 1))
                pool.sem_inc(g_src_seen, 1)
                for g in range(2):
                    nc.gpsimd.indirect_dma_start(
                        got_g[:, g, :], None, (P_dram if n == 0 else U_dram)[:, :],
                        bass.IndirectOffsetOnAxis(ap=src_g[:, g:g + 1], axis=0)).then_inc(g_got[g], 16)

            with if_unfit(pool):
                pool.wait_ge(g_start, 1)
                nc.gpsimd.iota(iota_g, [[1, NPAD]], base=0, channel_multiplier=0,
                               allow_small_or_imprecise_dtypes=True).then_inc(g_iota, 1)
                for n in range(4):
                    if n:
                        pool.wait_ge(g_stored, 16 * n)
                    with pool.Fori(0, NFULL) as k:
                        fetch(n, k, False)
                    fetch(n, NFULL, True)

        @block.scalar
        def _(act):
            act.wait_ge(padded, 1)
            for flat, tile, landed in ((src, src_s, src_in), (dst, dst_s, dst_in)):
                t3 = rows3(tile)
                act.dma_start(t3[:, 0:RB - 1, :],
                              flat[0:(RB - 1) * P * GE].rearrange("(b p c) -> p b c", p=P, c=GE)).then_inc(landed, 16)
                act.dma_start(t3[0:RLAST, RB - 1, :],
                              flat[(RB - 1) * P * GE:NFULL * GE].rearrange("(p c) -> p c", c=GE)).then_inc(landed, 16)
                act.dma_start(t3[RLAST:RLAST + 1, RB - 1, 0:TAIL],
                              flat[NFULL * GE:E].unsqueeze(0)).then_inc(landed, 16)
            act.wait_ge(src_in, 48)
            nc.scalar.copy(srcf_s, src_s).then_inc(srcf_done, 1)
            act.wait_ge(ln_var, 1)
            nc.scalar.activation(std, var, ACT.Sqrt, bias=epst[:, 0:1], scale=1.0 / F).then_inc(ln_std, 1)
            for g in range(2):
                act.wait_ge(src_turned, g + 1)
                nc.scalar.copy(srcT[:, :, g], ps[6 + g][:, 0:NFULL + BODY]).then_inc(srcT_done, 1)

            act.wait_ge(srcT_done, 2)
            nc.scalar.copy(gidx[:, :, :], srcT[:, 0:BODY, :]).then_inc(gidx_done, 1)

            for t in range(QUADS):
                act.wait_ge(hT_ps, t + 1)
                cols = slice(quad(t).start // 2 * P, -(-quad(t).stop // 2) * P)
                rows = P if quad(t).stop - quad(t).start > 1 else F
                nc.scalar.activation(hT[0:rows, cols], ps[t % 3][0:rows, 0:cols.stop - cols.start],
                                     ACT.Relu).then_inc(hT_sb, 1)
            act.wait_ge(ri_done, 1)
            nc.scalar.copy(rf_s, ri_s).then_inc(rf_done, 1)
            for t in range(QUADS):
                act.wait_ge(y3_ps, t + 1)
                n = quad(t).stop - quad(t).start
                nc.scalar.copy(y3[:, quad(t), :], nodes3(ps[t % 2][:, 0:n * F])).then_inc(y3_sb, 1)
            for i in range(6):
                act.wait_ge(turned, i + 1)
                tile = (rT, keyT, dlT)[i // 2]
                nc.scalar.copy(tile[:, :, i % 2], ps[2 + i][:, 0:NG]).then_inc(turned_sb, 1)
            act.wait_ge(cleared[3], 1)
            act.wait_ge(turned_sb, 6)
            for n in range(2):
                nc.scalar.copy(slab(NUMBERS + 2 + n), slab(NUMBERS + 5)).then_inc(cleared[2], 1)

            def group(k, par, third, first):
                act.wait_ge(eT_ps, k + 1)
                if not first or third == 2:
                    act.wait_ge(H_ps, k - 1)
                nc.scalar.copy(eT[:, par, :], ps_eT[par][:, 0:P]).then_inc(eT_sb, 1)
                act.wait_ge(H_ps, k + 1)
                if not first:
                    act.wait_ge(G_ps, k - 2)
                nc.scalar.activation(hid[:, third, :, 0:F],
                                     ps_H[par][:, 0:P].rearrange("p (g f) -> p g f", g=2),
                                     ACT.Relu).then_inc(hid_done, 1)

            def body(c, first):
                for k in range(BODY):
                    group(c * BODY + k, k % 2, k % 3, first and k < 3)
                    nc.scalar.copy(gidx[:, k, :], srcT[:, bass.ds(c * BODY + (BODY + k), 1), :].rearrange(
                        "p k g -> p (k g)")).then_inc(gidx_done, 1)

            body(0, True)
            with act.Fori(1, NBODY) as c:
                body(c, False)
            group(NFULL, 0, 0, False)
            act.wait_ge(deg_done, 1)
            nc.scalar.activation(dis, dis, ACT.Sqrt).then_inc(sqrt_done, 1)
            act.wait_ge(ln_var, 2)
            nc.scalar.activation(std, var, ACT.Sqrt, bias=epst[:, 0:1], scale=1.0 / F).then_inc(ln_std, 1)
            for t in range(PIECES):
                act.wait_ge(u_done, t + 1)
                nc.scalar.copy(U[:, piece(t), 0, :], u_first[:, piece(t), :]).then_inc(hi_done, 1)
            for t in range(PIECES):
                act.wait_ge(r_done, t + 1)
                nc.scalar.copy(U[:, piece(t), 1, :], u_first[:, piece(t), :]).then_inc(mid_done, 1)
            for b in range(NB):
                ins = nc.scalar.activation(acc[:, b, :], acc[:, b, :], ACT.Relu, scale=rstd[:, b:b + 1])
            ins.then_inc(h2_done, 1)
            def hidden_rows(k):
                act.wait_ge(g_eT_ps, k + 1)
                nc.scalar.copy(eT_g, ps[5][:, 0:P]).then_inc(g_eT_sb, 1)
                act.wait_ge(g_pre, k + 1)
                nc.scalar.activation(rows_g[:, :, 0:F], pre_g, ACT.Relu).then_inc(g_rows, 1)

            with if_unfit(act):
                with act.Fori(0, NFULL) as k:
                    hidden_rows(k)
                hidden_rows(NFULL)
                act.wait_ge(ln_var, 3)
                nc.scalar.activation(std, var, ACT.Sqrt, bias=epst[:, 0:1], scale=1.0 / F).then_inc(ln_std, 1)
                act.wait_ge(g_deg, 1)
                nc.scalar.activation(dis, dis, ACT.Sqrt).then_inc(g_sqrt, 1)

        @block.tensor
        def _(pe):
            pe.wait_ge(consts, 2)

            def turn_numbers(i, tile, g, done):
                t4 = tile.rearrange("p (b c g) -> p b c g", g=2, c=P)
                for b in range(RB):
                    ins = pe.transpose(ps[i][:, b * P:b * P + P], t4[:, b, :, g], ident[:, :])
                ins.then_inc(done, 1)

            pe.wait_ge(srcf_done, 1)
            for g in range(2):
                turn_numbers(6 + g, srcf_s, g, src_turned)

            def turn_rows(t):
                pe.wait_ge(hn_done, t + 1)
                if t >= 3:
                    pe.wait_ge(hT_sb, t - 2)
                for n, b in enumerate(range(quad(t).start, quad(t).stop, 2)):
                    two = h_s[:, b * F:min(b + 2, NB) * F]
                    ins = pe.transpose(ps[t % 3][0:two.shape[1], n * P:n * P + P], two, ident[:, :])
                ins.then_inc(hT_ps, 1)

            def pairs_of(t):
                for n, b in enumerate(range(quad(t).start, quad(t).stop, 2)):
                    rows = P if b + 1 < NB else F
                    yield n, rows, hT[0:rows, b // 2 * P:b // 2 * P + P]

            def node_part(t):
                pe.wait_ge(hT_sb, t + 1)
                if t >= 3:
                    pe.wait_ge(P_sb, t - 2)
                for n, rows, turned_rows in pairs_of(t):
                    ins = pe.matmul(ps[3 + t % 3][:, n * P:n * P + rows], turned_rows, W1n[0:rows, 0:rows],
                                    start=True, stop=True)
                ins.then_inc(nodes_ps, 1)

            for t in range(QUADS):
                turn_rows(t)
                if t == 1:
                    pe.wait_ge(w_in, 16 * LOADS)
                if t >= 1:
                    node_part(t - 1)
            node_part(QUADS - 1)
            pe.wait_ge(filled, 1)
            for t in range(QUADS):
                if t >= 2:
                    pe.wait_ge(y3_sb, t - 1)
                for n, rows, turned_rows in pairs_of(t):
                    into = ps[t % 2][:, n * P:n * P + rows]
                    pe.matmul(into, turned_rows, W3n[0:rows, 0:rows], start=True, stop=False)
                    ins = pe.matmul(into, ones_row, b3_row[:, 0:rows], start=False, stop=True)
                ins.then_inc(y3_ps, 1)
            pe.wait_ge(P_sb, QUADS)
            pe.wait_ge(srcT_done, 2)
            pe.wait_ge(rf_done, 1)
            for g in range(2):
                turn_numbers(2 + g, rf_s, g, turned)
            pe.wait_ge(nat_done, 1)
            for i in range(2, 6):
                turn_numbers(2 + i, (key_s, dl_s)[i // 2 - 1], i % 2, turned)
            pe.wait_ge(y3_sb, QUADS)
            for b in range(RB):
                ins = pe.transpose(ps[1][0:1, b * P:b * P + P], base_n[:, b:b + 1], ident[:, :])
            ins.then_inc(base_turned, 1)
            pe.transpose(ps[0][0:F, 0:F1], W2b[:, :], ident[0:F1, 0:F1]).then_inc(wfold_ps, 1)
            pe.wait_ge(wfold_sb, 1)
            pe.matmul(ps[0][0:F1, 128:128 + F], W2T[:, :], W3a[:, :], start=True, stop=True).then_inc(wfold_ps, 1)
            pe.wait_ge(base_read, 1)
            pe.wait_ge(wfold_sb, 2)
            pe.wait_ge(turned_sb, 6)

            def turn(k, par, slot, first):
                if not first:
                    pe.wait_ge(eT_sb, k - 1)
                pe.transpose(ps_eT[par][:, 0:P], e_ring[:, slot, :, :].rearrange("p g f -> p (g f)"),
                             ident[:, :]).then_inc(eT_ps, 1)

            def counts(k, par, first):
                pe.wait_ge(onehots, k + 1)
                if not first:
                    pe.wait_ge(A_added, k - 1)
                for g in range(2):
                    ins = pe.matmul(ps_A[par][:, 0:KEYS], oh_r[:, par, g, :], oh_key[:, par, g, :],
                                    start=(g == 0), stop=(g == 1))
                ins.then_inc(A_ps, 1)

            def hidden(c, k, par, slot, first):
                pe.wait_ge(eT_sb, k + 1)
                if not first:
                    pe.wait_ge(hid_done, k - 1)
                pe.matmul(ps_H[par][:, 0:P], eT[:, par, :], W1e[:, :], start=True, stop=False)
                pe.wait_ge(gathered[slot], c * 32 + 32)
                pe.matmul(ps_H[par][:, 0:P], ident[:, :], g_ring[:, slot, :, :].rearrange("p g f -> p (g f)"),
                          start=False, stop=True).then_inc(H_ps, 1)

            def sums(k, par, third, first):
                pe.wait_ge(hid_done, k + 1)
                if not first:
                    pe.wait_ge(G_added, k - 1)
                for g in range(2):
                    ins = pe.matmul(ps_G[par][0:F1, 0:W], hid[:, third, g, :], oh_w[:, third, g, :],
                                    start=(g == 0), stop=(g == 1))
                ins.then_inc(G_ps, 1)

            def body(c, first):
                for k in range(BODY):
                    if k % HALF == 0:
                        pe.wait_ge(e_in[k // HALF], c * 16 + 16)
                    turn(c * BODY + k, k % 2, k, first and k < 2)
                    if not (first and k < 2):
                        sums(c * BODY + (k - 2), k % 2, (k - 2) % 3, first and k < 4)
                    counts(c * BODY + k, k % 2, first and k < 2)
                    hidden(c, c * BODY + k, k % 2, k, first and k < 2)

            body(0, True)
            with pe.Fori(1, NBODY) as c:
                body(c, False)
            pe.wait_ge(e_in[0], 16 * (NBODY + 2))
            turn(NFULL, 0, 0, False)
            sums(NFULL - 2, 0, 1, False)
            counts(NFULL, 0, False)
            hidden(NBODY, NFULL, 0, 0, False)
            sums(NFULL - 1, 1, 2, False)
            sums(NFULL, 0, 0, False)
            pe.wait_ge(A_added, NG)
            pe.wait_ge(G_added, NG)
            for t in range(PIECES):
                for j in range(PIECE):
                    b = t * PIECE + j
                    ins = pe.matmul(ps[t][:, j * F1:(j + 1) * F1], aggT[:, b * P:b * P + P],
                                    W23[:, :], start=True, stop=True)
                ins.then_inc(z_ps, 1)
            with pe.Fori(0, LAYERS) as layer:
                for b in range(NB):
                    pe.wait_ge(V_read, layer * NB + (b + 1))
                    for q in range(NB):
                        if b == 0 and q % PIECE == 0:
                            pe.wait_ge(U_done, layer * PIECES + (q // PIECE + 1))
                        ins = pe.matmul(ps[b % PIECE][:, 0:3 * F], A[:, q, b * P:b * P + P],
                                        U[:, q, :, :].rearrange("p s f -> p (s f)"),
                                        start=(q == 0), stop=(q == NB - 1))
                    ins.then_inc(V_ps, 1)
            pe.wait_ge(unfit_done, 1)
            pe.matmul(ps[5][0:1, 0:1], unfit[:, 0:1], ones[:, :], start=True, stop=True).then_inc(unfit_ps, 1)

            def scatter(n, k, last_one):
                if n == 0:
                    pe.wait_ge(g_e, 16 * STEP if last_one else k * 16 + 16)
                    pe.transpose(ps[5][:, 0:P], e_g.rearrange("p g f -> p (g f)"), ident[:, :]).then_inc(g_eT_ps, 1)
                    pe.wait_ge(g_eT_sb, k + 1)
                    pe.matmul(ps[6][:, 0:P], eT_g, W1e[:, :], start=True, stop=True).then_inc(g_H_ps, 1)
                    pe.wait_ge(g_rows, k + 1)
                else:
                    for g in range(2):
                        pe.wait_ge(g_got[g], k * 16 + 16 * (NG * n + 1))
                pe.wait_ge(g_onehot, k + (NG * n + 1))
                width = F1 if n == 0 else F
                for b in range(NB):
                    at = b % PIECE * F1
                    for g in range(2):
                        ins = pe.matmul(ps[b // PIECE][:, at:at + width], oh_g[:, g, b * P:b * P + P],
                                        (rows_g if n == 0 else got_g)[:, g, :], start=(g == 0), stop=(g == 1))
                ins.then_inc(g_prod, 1)

            with if_unfit(pe):
                for n in range(4):
                    with pe.Fori(0, NFULL) as k:
                        scatter(n, k, False)
                    scatter(n, NFULL, True)
                    if n == 0:
                        pe.wait_ge(g_freed, NG + 1)
                        for b in range(NB):
                            pe.transpose(ps[5][0:F1, 0:P], sums_g[:, b, :], ident[:, :]).then_inc(g_aggT_ps, 1)
                            pe.wait_ge(g_aggT_sb, b + 1)
                            pe.matmul(ps[6][:, 0:F1], aggT[:, b * P:b * P + P], W23[:, :],
                                      start=True, stop=True).then_inc(g_z_ps, 1)
                            pe.wait_ge(g_z_sb, b + 1)

        @block.vector
        def _(dve):
            chain = [0]

            def link(ins):
                chain[0] += 1
                ins.then_inc(link_d, 1)
                dve.wait_ge(link_d, chain[0])

            def per_node(t, n=NB):
                return t.unsqueeze(2).to_broadcast([P, n, F])

            nc.vector.memset(acc[:, NB - 1, :], 0.0)
            nc.vector.memset(rows3(src_s)[:, RB - 1, :], 0)
            nc.vector.memset(rows3(dst_s)[:, RB - 1, :], FAR).then_inc(padded, 1)
            nc.vector.memset(epst[:], EPS)
            nc.vector.memset(W1e[:], 0.0)
            nc.vector.memset(after_hT[:, 0:2 * P], 0.0)
            nc.vector.memset(ones[:], 1.0)
            nc.vector.memset(hid[:], 1.0)
            nc.vector.memset(ones_row, 1.0)
            link(nc.vector.memset(W23[:], 0.0))
            nc.vector.memset(W23[F:F1, F:F1], 1.0).then_inc(filled, 1)
            nc.vector.memset(slab(NUMBERS + 5), 0.0).then_inc(cleared[3], 1)

            def deviations(xt, n):
                for b in range(NB):
                    ins = nc.vector.bn_stats(bn[:, b, :], xt[:, b, :])
                link(ins)
                nc.vector.tensor_tensor(mean, bn[:, :, 1], bn[:, :, 4], ALU.add)
                nc.vector.tensor_tensor(var, bn[:, :, 2], bn[:, :, 5], ALU.add)
                link(nc.vector.tensor_tensor(gap, bn[:, :, 1], bn[:, :, 4], ALU.subtract))
                nc.vector.tensor_scalar(mean, mean, 0.5, None, ALU.mult)
                link(nc.vector.scalar_tensor_tensor(out=gap, in0=gap, scalar=F / 4.0, in1=gap,
                                                    op0=ALU.mult, op1=ALU.mult))
                nc.vector.tensor_tensor(var, var, gap, ALU.add).then_inc(ln_var, 1)
                dve.wait_ge(ln_std, n)
                link(nc.vector.reciprocal(rstd, std))

            dve.wait_ge(x_in, 32)
            deviations(acc, 1)

            def centre(t):
                n = quad(t).stop - quad(t).start
                nc.vector.tensor_tensor(nodes3(h_s)[:, quad(t), :], acc[:, quad(t), :],
                                        per_node(mean[:, quad(t)], n), ALU.subtract).then_inc(hn_sub, 1)

            centre(0)
            for t in range(QUADS):
                if t + 1 < QUADS:
                    centre(t + 1)
                dve.wait_ge(hn_sub, t + 1)
                part = nodes3(h_s)[:, quad(t), :]
                nc.vector.tensor_tensor(part, part, per_node(rstd[:, quad(t)], quad(t).stop - quad(t).start),
                                        ALU.mult).then_inc(hn_done, 1)
            dve.wait_ge(src_in, 48)
            nc.vector.tensor_scalar(ri_s, src_s, P - 1, None, ALU.bitwise_and).then_inc(ri_done, 1)
            dve.wait_ge(dst_in, 48)
            link(nc.vector.tensor_reduce(base_n[:], rows3(dst_s), AX.X, ALU.min))
            for t in range(QUADS):
                dve.wait_ge(nodes_ps, t + 1)
                n = quad(t).stop - quad(t).start
                nc.vector.tensor_tensor(nodes3(P_s)[:, quad(t), :], nodes3(ps[3 + t % 3][:, 0:n * F]),
                                        b1_all.unsqueeze(1).to_broadcast([P, n, F]), ALU.add).then_inc(P_sb, 1)
            link(nc.vector.tensor_tensor(rows3(key_s), rows3(dst_s),
                                         base_n[:].unsqueeze(2).to_broadcast([P, RB, GE]), ALU.subtract))
            link(nc.vector.tensor_scalar(dl_s, key_s, W - 0.5, NO_SLOT, ALU.is_gt, ALU.mult))
            nc.vector.tensor_reduce(unfit[:, 0:1], dl_s, AX.X, ALU.add)
            dve.wait_ge(rf_done, 1)
            link(nc.vector.scalar_tensor_tensor(out=dl_s, in0=key_s, scalar=NO_SLOT, in1=dl_s,
                                                op0=ALU.min, op1=ALU.max))
            link(nc.vector.tensor_tensor(key_s, srcf_s, rf_s, ALU.subtract))
            nc.vector.scalar_tensor_tensor(out=key_s, in0=key_s, scalar=float(W) / P, in1=dl_s,
                                           op0=ALU.mult, op1=ALU.add).then_inc(nat_done, 1)
            nc.vector.memset(aggT[:], 0.0)
            dve.wait_ge(P_out, 16 * QUADS)
            dve.wait_ge(y3_ps, QUADS)
            nc.vector.memset(slab(ROWS, NB - ROWS), 0.0)
            dve.wait_ge(base_turned, 1)
            nc.vector.tensor_copy(base_row[:], ps[1][0:1, :]).then_inc(base_read, 1)
            dve.wait_ge(wfold_ps, 1)
            nc.vector.tensor_copy(W2T[:, :], ps[0][0:F, 0:F1]).then_inc(wfold_sb, 1)
            dve.wait_ge(wfold_ps, 2)
            nc.vector.tensor_copy(W23[:, 0:F], ps[0][0:F1, 128:128 + F]).then_inc(wfold_sb, 1)
            dve.wait_ge(turned_sb, 6)
            link(nc.vector.memset(slab(NUMBERS, 2), 0.0))
            dve.wait_ge(consts, 3)
            dve.wait_ge(base_read, 1)

            def make_onehots(k, par, third, first):
                if not first:
                    dve.wait_ge(G_ps, k - 2)
                if not first or third == 2:
                    dve.wait_ge(A_ps, k - 1)
                nc.vector.tensor_tensor(
                    oh_w[:, third, :, :], iota_w[:].unsqueeze(1).to_broadcast([P, 2, W]),
                    dlT[:, bass.ds(k, 1), :].rearrange("p k g -> p (k g)").unsqueeze(2).to_broadcast([P, 2, W]),
                    ALU.is_equal)
                for g in range(2):
                    nc.vector.tensor_scalar(oh_r[:, par, g, :], iota_r[:],
                                            rT[:, bass.ds(k, 1), g], None, ALU.is_equal)
                    ins = nc.vector.tensor_scalar(oh_key[:, par, g, :], iota_key[:],
                                                  keyT[:, bass.ds(k, 1), g], None, ALU.is_equal)
                ins.then_inc(onehots, 1)

            def add_counts(k, par, base, first):
                dve.wait_ge(A_ps, k + 1)
                if first:
                    dve.wait_ge(cleared[0], 1)
                    dve.wait_ge(cleared[1], 1)
                    dve.wait_ge(cleared[2], 2)
                else:
                    dve.wait_ge(A_added, k)
                Aw = A[:, :, bass.ds(base, W)]
                nc.vector.tensor_tensor(Aw, Aw, ps_A[par][:, 0:KEYS].rearrange("p (q w) -> p q w", w=W),
                                        ALU.add).then_inc(A_added, 1)

            def add_sums(k, par, base, first):
                dve.wait_ge(G_ps, k + 1)
                if not first:
                    dve.wait_ge(G_added, k)
                Gw = aggT[:, bass.ds(base, W)]
                nc.vector.tensor_tensor(Gw, Gw, ps_G[par][0:F1, 0:W], ALU.add).then_inc(G_added, 1)

            def load_bases(k, n):
                _, vals = nc.values_load_multi_w_load_instructions(
                    base_row[0:1, bass.ds(k, n)], engines=[mybir.EngineType.DVE], min_val=0, max_val=NPAD - W,
                    skip_runtime_bounds_check_because="a destination is below N, and N - 1 + W is within the padded width")
                return vals

            def body(c, first):
                vals = load_bases(0, BODY) if first else load_bases(c * BODY - 2, BODY + 2)
                ahead = 0 if first else 2
                for k in range(BODY):
                    make_onehots(c * BODY + k, k % 2, k % 3, first and k < 3)
                    if not (first and k == 0):
                        add_counts(c * BODY + (k - 1), (k + 1) % 2, vals[k - 1 + ahead], first and k == 1)
                    if not (first and k < 2):
                        add_sums(c * BODY + (k - 2), k % 2, vals[k - 2 + ahead], first and k == 2)

            body(0, True)
            with dve.Fori(1, NBODY) as c:
                body(c, False)
            vals = load_bases(NFULL - 2, 3)
            dve.wait_ge(eT_ps, NFULL - BODY + 1)
            nc.vector.memset(e_ring[:, 0, :, :], 0.0).then_inc(padded, 1)
            make_onehots(NFULL, 0, 0, False)
            add_counts(NFULL - 1, 1, vals[1], False)
            add_sums(NFULL - 2, 0, vals[0], False)
            add_counts(NFULL, 0, vals[2], False)
            add_sums(NFULL - 1, 1, vals[1], False)
            add_sums(NFULL, 0, vals[2], False)

            def update_sum(t):
                dve.wait_ge(z_ps, t + 1)
                z = ps[t][:, 0:PIECE * F1].rearrange("p (j c) -> p j c", c=F1)
                nc.vector.tensor_copy(deg[:, piece(t)], z[:, :, F])
                nc.vector.tensor_tensor(y3[:, piece(t), :], y3[:, piece(t), :], z[:, :, 0:F],
                                        ALU.add).then_inc(V_read, 1)

            def residual(t):
                dve.wait_ge(V_read, t + 1)
                nc.vector.scalar_tensor_tensor(out=y3[:, piece(t), :], in0=y3[:, piece(t), :], scalar=0.0,
                                               in1=acc[:, piece(t), :], op0=ALU.max, op1=ALU.add).then_inc(x2_sum, 1)

            update_sum(0)
            for t in range(PIECES):
                if t + 1 < PIECES:
                    update_sum(t + 1)
                residual(t)
            nc.vector.tensor_scalar(dis, deg, 1.0, None, ALU.max).then_inc(deg_done, 1)
            dve.wait_ge(x2_sum, PIECES)
            deviations(y3, 2)
            dve.wait_ge(sqrt_done, 1)
            link(nc.vector.reciprocal(dis, dis))
            link(nc.vector.scalar_tensor_tensor(out=dis, in0=deg, scalar=0.5, in1=dis, op0=ALU.is_gt, op1=ALU.mult))
            nc.vector.tensor_tensor(dis2, dis, dis, ALU.mult)
            link(nc.vector.tensor_tensor(gap, dis, rstd, ALU.mult))
            for t in range(PIECES):
                nc.vector.tensor_tensor(acc[:, piece(t), :], y3[:, piece(t), :],
                                        per_node(mean[:, piece(t)], PIECE), ALU.subtract).then_inc(xc_done, 1)
            for t in range(PIECES):
                dve.wait_ge(xc_done, t + 1)
                nc.vector.scalar_tensor_tensor(out=u_first[:, piece(t), :], in0=acc[:, piece(t), :], scalar=0.0,
                                               in1=per_node(gap[:, piece(t)], PIECE),
                                               op0=ALU.max, op1=ALU.mult).then_inc(u_done, 1)
            for t in range(PIECES):
                dve.wait_ge(hi_done, t + 1)
                nc.vector.tensor_tensor(u_first[:, piece(t), :], u_first[:, piece(t), :], U[:, piece(t), 0, :],
                                        ALU.subtract).then_inc(r_done, 1)
            for t in range(PIECES):
                dve.wait_ge(mid_done, t + 1)
                nc.vector.tensor_tensor(U[:, piece(t), 2, :], u_first[:, piece(t), :], U[:, piece(t), 1, :],
                                        ALU.subtract).then_inc(U_done, 1)
            link(nc.vector.tensor_scalar(mean, deg, MAX_EXACT + 0.5, NO_SLOT, ALU.is_gt, ALU.mult))
            link(nc.vector.tensor_reduce(unfit[:, 1:2], mean, AX.X, ALU.add))
            nc.vector.tensor_tensor(unfit[:, 0:1], unfit[:, 0:1], unfit[:, 1:2], ALU.add).then_inc(unfit_done, 1)
            dve.wait_ge(h2_done, 1)

            def read_product(layer, b):
                dve.wait_ge(V_ps, layer * NB + (b + 1))
                nc.vector.tensor_reduce(v[:, b % 2, :], ps[b % PIECE][:, 0:3 * F].rearrange(
                    "p (s f) -> p f s", f=F), AX.X, ALU.add).then_inc(V_read, 1)
                dve.wait_ge(V_read, layer * NB + (b + 1 + PIECES))
                return nc.vector.scalar_tensor_tensor(out=acc[:, b, :], in0=v[:, b % 2, :], scalar=dis[:, b:b + 1],
                                                      in1=acc[:, b, :], op0=ALU.mult, op1=ALU.add)

            def split_next(layer, b):
                def step(i, ins):
                    ins.then_inc(split_done, 1)
                    dve.wait_ge(split_done, layer * (NB * SPLIT_STEPS) + (b * SPLIT_STEPS + i))
                vb, rb, scale = v[:, b % 2, :], rem[:, b % 2, :], dis2[:, b:b + 1]
                hi, mid, lo = (U_next[:, b, s, :] for s in range(3))
                step(1, nc.vector.tensor_scalar(hi, vb, scale, None, ALU.mult))
                step(2, nc.vector.scalar_tensor_tensor(out=rb, in0=vb, scalar=scale, in1=hi,
                                                       op0=ALU.mult, op1=ALU.subtract))
                step(3, nc.vector.tensor_copy(mid, rb))
                step(4, nc.vector.tensor_tensor(lo, rb, mid, ALU.subtract))

            def hand_over(t):
                nc.vector.tensor_copy(U[:, piece(t), :, :], U_next[:, piece(t), :, :]).then_inc(U_done, 1)

            with dve.Fori(0, LAYERS - 1) as layer:
                for b in range(NB - 1):
                    read_product(layer, b)
                    split_next(layer, b)
                read_product(layer, NB - 1)
                for t in range(PIECES - 1):
                    hand_over(t)
                split_next(layer, NB - 1)
                hand_over(PIECES - 1)
            for b in range(NB):
                ins = read_product(LAYERS - 1, b)
                if b % PIECE == PIECE - 1:
                    t = b // PIECE
                    link(ins)
                    nc.vector.scalar_tensor_tensor(out=acc[:, piece(t), :], in0=acc[:, piece(t), :], scalar=0.25,
                                                   in1=y3[:, piece(t), :], op0=ALU.mult,
                                                   op1=ALU.add).then_inc(out_done, 1)
            dve.wait_ge(unfit_ps, 1)
            nc.vector.tensor_scalar(flag[:], ps[5][0:1, 0:1], NO_SLOT * (GE - TAIL + 0.5), None,
                                    ALU.is_gt).then_inc(flag_done, 1)

            def general():
                link(nc.vector.memset(rows_g, 1.0))
                link(nc.vector.memset(x2_g[:, NB - 1, :], 0.0))
                link(nc.vector.memset(sums_g, 0.0))
                nc.vector.engine_nop().then_inc(g_start, 1)
                nc.vector.engine_nop().then_inc(g_freed, 1)
                dve.wait_ge(g_iota, 1)

                def onehot_and_sum(n, k, last_one):
                    dve.wait_ge(g_dst, 16 * STEP * (n + 1) if last_one else k * 16 + 16 * (STEP * n + 1))
                    nc.vector.tensor_copy(dstf_g, dst_g).then_inc(g_dst_sb, 1)
                    dve.wait_ge(g_dst_sb, k + (n * NG + 1))
                    for g in range(2):
                        ins = nc.vector.tensor_scalar(oh_g[:, g, :], iota_g, dstf_g[:, g:g + 1], None, ALU.is_equal)
                    ins.then_inc(g_onehot, 1)
                    if n == 0:
                        dve.wait_ge(g_H_ps, k + 1)
                        for g in range(2):
                            dve.wait_ge(g_got[g], k * 16 + 16)
                        nc.vector.tensor_tensor(pre_g, ps[6][:, 0:P].rearrange("p (g f) -> p g f", g=2),
                                                got_g, ALU.add).then_inc(g_pre, 1)
                    width = F1 if n == 0 else F
                    dve.wait_ge(g_prod, k + (n * NG + 1))
                    for t in range(NB // PIECE):
                        part = ps[t][:, 0:PIECE * F1].rearrange("p (j c) -> p j c", c=F1)[:, :, 0:width]
                        into = sums_g[:, t * PIECE:(t + 1) * PIECE, 0:width]
                        ins = nc.vector.tensor_tensor(into, into, part, ALU.add)
                    ins.then_inc(g_freed, 1)
                    dve.wait_ge(g_freed, k + (n * NG + 2))

                for n in range(4):
                    with dve.Fori(0, NFULL) as k:
                        onehot_and_sum(n, k, False)
                    nc.vector.memset(src_g, 0)
                    nc.vector.memset(e_g, 0.0)
                    nc.vector.memset(dst_g, FAR).then_inc(g_padded, 1)
                    onehot_and_sum(n, NFULL, True)
                    if n == 0:
                        dve.wait_ge(g_node_in, 48)
                        for b in range(NB):
                            dve.wait_ge(g_aggT_ps, b + 1)
                            nc.vector.tensor_copy(aggT[:, b * P:b * P + P], ps[5][0:F1, 0:P]).then_inc(g_aggT_sb, 1)
                            dve.wait_ge(g_z_ps, b + 1)
                            nc.vector.tensor_copy(deg[:, b:b + 1], ps[6][:, F:F1])
                            nc.vector.tensor_tensor(y3_g[:, b, :], y3_g[:, b, :], ps[6][:, 0:F],
                                                    ALU.add).then_inc(g_z_sb, 1)
                        dve.wait_ge(g_z_sb, NB)
                        nc.vector.tensor_scalar(dis, deg, 1.0, None, ALU.max).then_inc(g_deg, 1)
                        link(nc.vector.scalar_tensor_tensor(out=x2_g, in0=y3_g, scalar=0.0, in1=x2_g,
                                                            op0=ALU.max, op1=ALU.add))
                        deviations(x2_g, 3)
                        link(nc.vector.tensor_tensor(acc_g, x2_g, per_node(mean), ALU.subtract))
                        link(nc.vector.scalar_tensor_tensor(out=acc_g, in0=acc_g, scalar=0.0, in1=per_node(rstd),
                                                            op0=ALU.max, op1=ALU.mult))
                        dve.wait_ge(g_sqrt, 1)
                        link(nc.vector.reciprocal(dis, dis))
                        link(nc.vector.scalar_tensor_tensor(out=dis, in0=deg, scalar=0.5, in1=dis,
                                                            op0=ALU.is_gt, op1=ALU.mult))
                        nc.vector.tensor_tensor(u_g, acc_g, per_node(dis), ALU.mult).then_inc(g_u, 1)
                    else:
                        link(nc.vector.tensor_tensor(sq_g, sums_g[:, :, 0:F], per_node(dis), ALU.mult))
                        link(nc.vector.tensor_tensor(acc_g, acc_g, sq_g, ALU.add))
                        if n < 3:
                            dve.wait_ge(g_stored, 16 * n)
                            nc.vector.tensor_tensor(u_g, sq_g, per_node(dis), ALU.mult).then_inc(g_u, 1)
                        else:
                            nc.vector.scalar_tensor_tensor(out=acc_g, in0=acc_g, scalar=0.25, in1=x2_g,
                                                           op0=ALU.mult, op1=ALU.add).then_inc(g_u, 1)
                    if n < 3:
                        link(nc.vector.memset(sums_g, 0.0))

            with if_unfit(dve):
                general()


_INS = ['x', 'src', 'dst', 'edge_attr_64', 'L0_gnn_W1', 'L0_gnn_b1', 'L0_gnn_W2', 'L0_gnn_b2', 'L0_gnn_W3', 'L0_gnn_b3']


def kernel(**inputs):
    import numpy as _np
    import concourse.bacc as _bacc
    from concourse import mybir as _mybir
    from concourse.bass_utils import run_bass_kernel_spmd as _run

    nc = _bacc.Bacc("TRN2", target_bir_lowering=False, num_devices=1)
    arrays, args = {}, []
    for name in _INS:
        a = _np.ascontiguousarray(inputs[name])
        arrays[f"in_{name}_dram"] = a
        args.append(nc.dram_tensor(f"in_{name}_dram", a.shape, _mybir.dt.from_np(a.dtype), kind="ExternalInput").ap())
    args.append(nc.dram_tensor("out_0_dram", inputs['x'].shape, F32, kind="ExternalOutput").ap())
    gnn_and_propagation(nc, *args)
    r = _run(nc, [arrays], core_ids=[0])
    return r.results[0]["out_0_dram"]
```

```python
from contextlib import ExitStack

import concourse.bass as bass
from concourse import mybir

ALU = mybir.AluOpType
ACT = mybir.ActivationFunctionType
AX = mybir.AxisListType
F32 = mybir.dt.float32
F16 = mybir.dt.float16
BF16 = mybir.dt.bfloat16
I32 = mybir.dt.int32

P = 128
F = 64
W = 12
HALF = 3
RING = 2 * HALF
BODY = 12
ONE = BODY - 2
MAX_EXACT = 256
FAR = 1 << 20
NO_SLOT = 1000.0
EPS = 1e-5
PIECE = 5
QUAD = 4
LAYERS = 3
HOTS = (3, 2)
SPLIT_STEPS = 4


def gnn_and_propagation(nc, x, src, dst, edge, W1, b1, W2, b2, W3, b3, out):
    N, E = x.shape[0], src.shape[0]
    NB = -(-N // P)
    NPAD = NB * P
    NLAST = N - (NB - 1) * P
    GE = 2 * P
    NG = -(-E // GE)
    NFULL = E // GE
    TAIL = E - NFULL * GE
    NBODY = (NFULL - RING) // BODY
    SETS = ONE
    RB = -(-NG // P)
    RLAST = NFULL - (RB - 1) * P
    KEYS = NB * W
    QUADS = -(-NB // QUAD)
    F1 = F + 1
    assert RING + NBODY * BODY == NFULL and SETS // 2 * sum(HOTS) == NB and NG == NFULL + 1 and TAIL > P and TAIL % 2 == 1 and NB % PIECE == 0
    assert N - 1 + W <= NPAD and KEYS <= 512 and NFULL + RING <= RB * P

    with ExitStack() as ctx:
        def sb(name, shape, dt, stack=ctx):
            return stack.enter_context(nc.sbuf_tensor(name, shape, dt))

        def sem(name):
            return ctx.enter_context(nc.semaphore(name))

        P_dram = nc.dram_tensor("node_part", (NPAD, F), F32).ap()
        y3_dram = nc.dram_tensor("node_update", (P, NB, F), F32).ap()
        x_dram = nc.dram_tensor("node_features", (P, NB, F), F32).ap()
        U_dram = nc.dram_tensor("scaled", (NPAD, F), F32).ap()

        A = sb("A", [P, NB, NPAD], BF16)

        def slab(q, n=1, dt=F32):
            return A[:, q:q + n, :].rearrange("p a b -> p (a b)").bitcast(dt)

        NS = RB * GE
        NUMBERS, ROWS = 15, 21

        def numbers(i, dt=F32):
            return slab(NUMBERS, 5, dt)[:, i * NS:(i + 1) * NS]

        src_s, dst_s, ri_s = (numbers(i, I32) for i in range(3))
        srcf_s, rf_s, key_s, dl_s = (numbers(i) for i in range(3, 7))
        fold_place = slab(NUMBERS, 5)[:, 7 * NS:7 * NS + 4 * F]
        W2b = fold_place[0:F1, 0:F]
        W3a = fold_place[0:F, F:2 * F]
        W2T = fold_place[0:F, 2 * F:2 * F + F1]
        rows_place = slab(ROWS, 2)
        PAIRS = -(-NB // 2)
        hT = rows_place[:, 0:PAIRS * P]
        after_hT = rows_place[:, PAIRS * P:]
        W1n, W3n = after_hT[:, 0:P], after_hT[:, P:2 * P]
        b1_all = after_hT[:, 2 * P:2 * P + F]
        b3_row = after_hT[0:1, 3 * P:4 * P]
        ones_row = after_hT[0:1, 4 * P:5 * P]
        bn_start = after_hT[:, 5 * P:5 * P + 6 * NB].rearrange("p (b s) -> p b s", s=6)
        P_s, h_s = slab(23), slab(24)
        y3_s = h_s

        node3 = lambda t: t.rearrange("p (b f) -> p b f", f=F)
        x2_g, acc_g, y3_g, sq_g, u_g = (node3(slab(q)) for q in (0, 1, 2, 12, 13))
        sums_g = slab(3, 2)[:, 0:NB * F1].rearrange("p (b c) -> p b c", c=F1)
        iota_g = slab(5, 2)
        oh_g = slab(7, 4).rearrange("p (g n) -> p g n", g=2)
        small_g = slab(11)
        e_g = small_g[:, 0:2 * F].rearrange("p (g f) -> p g f", g=2)
        got_g = small_g[:, 2 * F:4 * F].rearrange("p (g f) -> p g f", g=2)
        eT_g = small_g[:, 4 * F:6 * F]
        pre_g = small_g[:, 6 * F:8 * F].rearrange("p (g f) -> p g f", g=2)
        rows_g = small_g[:, 8 * F:8 * F + 2 * F1].rearrange("p (g c) -> p g c", g=2)
        dstf_g = small_g[:, 12 * F:12 * F + 2]
        src_g = slab(11, 1, I32)[:, 13 * F:13 * F + 2]
        dst_g = slab(11, 1, I32)[:, 14 * F:14 * F + 2]

        ident = sb("ident", [P, P], F32)
        ones = sb("ones", [P, 1], F32)
        W1e = sb("W1e", [P, P], F32)
        W23 = sb("W23", [F1, F1], F32)
        stat = sb("stat", [P, 8, NB], F32)
        mean, var, std, rstd, deg, dis, dis2, gap = (stat[:, i, :] for i in range(8))
        epst = sb("epst", [P, 1], F32)
        unfit = sb("unfit", [P, 2], F32)
        flag = sb("flag", [1, 1], I32)
        base_n = sb("base_n", [P, RB], F32)
        base_row = sb("base_row", [1, RB * P], I32)
        aggT = sb("aggT", [F1, NPAD], F32)
        nodes = sb("nodes", [P, 2 * NB * F], F32)
        acc = nodes[:, 0:NB * F].rearrange("p (b f) -> p b f", f=F)
        y3 = nodes[:, NB * F:].rearrange("p (b f) -> p b f", f=F)
        PARTS = NB * 3 * F // 2
        P_parts = nodes[:, 0:PARTS].bitcast(BF16).rearrange("p (b s f) -> p b s f", s=3, f=F)
        oh_n = nodes[:, PARTS:PARTS + sum(HOTS) * P].bitcast(BF16).rearrange("p (n g c) -> p n g c", g=2, c=P)
        node_of = nodes[:, PARTS + sum(HOTS) * P:][:, 0:NB]

        edge_phase = ExitStack()

        def eb(name, shape, dt):
            return sb(name, shape, dt, edge_phase)

        srcT = eb("srcT", [P, NFULL + RING, 2], I32)
        src_all = eb("src_all", [P, GE], I32)
        keyT = eb("keyT", [P, NG, 2], F16)
        rT = eb("rT", [P, NG, 2], BF16)
        dlT = eb("dlT", [P, NG, 2], BF16)
        iota_key = eb("iota_key", [P, KEYS], F16)
        iota_r, iota_w = iota_key[:, 0:P], iota_key[:, 0:W]
        e_ring = eb("e_ring", [P, RING, 2, F], F32)
        g_ring = eb("g_ring", [P, RING, 2, F], F32)
        gidx = eb("gidx", [P, RING, 2], I32)
        eT = eb("eT", [P, 2, P], F32)
        hid = eb("hid", [P, 3, 2, F1], F32)
        oh_key = eb("oh_key", [P, 2, 2, KEYS], BF16)
        oh_r = eb("oh_r", [P, 2, 2, P], BF16)
        oh_w = eb("oh_w", [P, 3, 2, W], F32)
        edge_phase.close()

        prop_phase = ExitStack()

        def pb(name, shape, dt):
            return sb(name, shape, dt, prop_phase)

        U = pb("U", [P, NB, 3, F], BF16)
        U_next = pb("U_next", [P, NB, 3, F], BF16)
        v = pb("v", [P, 2, F], F32)
        rem = pb("rem", [P, 2, F], F32)
        prop_phase.close()
        bn_later = U[:].rearrange("p b s f -> p (b s f)").bitcast(F32)[:, 0:6 * NB].rearrange(
            "p (b s) -> p b s", s=6)
        u_first = U_next[:].rearrange("p b s f -> p (b s f)").bitcast(F32)[:, 0:NB * F].rearrange(
            "p (b f) -> p b f", f=F)

        ps = [ctx.enter_context(nc.psum_tensor(f"ps{i}", [P, 512], F32)) for i in range(8)]
        ps_eT, ps_G, ps_H, ps_A = ps[6], ps[0:2], ps[2:4], ps[4:6]
        ps_parts = ps[7][:].rearrange("p (g s f) -> p g s f", g=2, s=4)

        padded = sem("padded")
        x_in = [sem(f"x_in{i}") for i in range(3)]
        src_in, dst_in, w_in = sem("src_in"), sem("dst_in"), sem("w_in")
        consts = sem("consts")
        cleared = [sem(f"cleared{i}") for i in range(4)]
        copied_zeros = sem("copied_zeros")
        filled = sem("filled")
        link_d = sem("link_d")
        ln_var, ln_std = sem("ln_var"), sem("ln_std")
        hn_sub, hn_done = sem("hn_sub"), sem("hn_done")
        hT_ps, hT_sb = sem("hT_ps"), sem("hT_sb")
        nodes_ps, P_sb, y3_ps, y3_sb = sem("nodes_ps"), sem("P_sb"), sem("y3_ps"), sem("y3_sb")
        P_out, y3_out = sem("P_out"), sem("y3_out")
        srcf_done, ri_done, rf_done, nat_done = (sem(n) for n in ("srcf_done", "ri_done", "rf_done", "nat_done"))
        src_turned, srcT_done = sem("src_turned"), sem("srcT_done")
        turned, turned_sb = sem("turned"), sem("turned_sb")
        base_turned, base_read = sem("base_turned"), sem("base_read")
        wfold_ps, wfold_sb = sem("wfold_ps"), sem("wfold_sb")
        e_in = [sem(f"e_in{i}") for i in range(2)]
        gathered = [sem(f"gathered{i}") for i in range(RING)]
        gidx_done, gidx_seen = sem("gidx_done"), sem("gidx_seen")
        eT_ps, eT_sb = sem("eT_ps"), sem("eT_sb")
        H_ps, hid_done = sem("H_ps"), sem("hid_done")
        onehots = sem("onehots")
        last_in = sem("last_in")
        src_all_in = sem("src_all_in")
        hi_P, rest_P, mid_P, parts_P = (sem(n) for n in ("hi_P", "rest_P", "mid_P", "parts_P"))
        squared = sem("squared")
        squared_seen = sem("squared_seen")
        hot_act, hot_dve = sem("hot_act"), sem("hot_dve")
        hot_used = sem("hot_used")
        part_sum = sem("part_sum")
        x_out, x_again, y3_again = sem("x_out"), sem("x_again"), sem("y3_again")
        A_ps, A_added = sem("A_ps"), sem("A_added")
        G_ps, G_added = sem("G_ps"), sem("G_added")
        z_ps, x2_sum = sem("z_ps"), sem("x2_sum")
        deg_done, sqrt_done = sem("deg_done"), sem("sqrt_done")
        xc_done, h2_done = sem("xc_done"), sem("h2_done")
        u_done, hi_done, r_done, mid_done = (sem(n) for n in ("u_done", "hi_done", "r_done", "mid_done"))
        U_done = sem("U_done")
        V_ps, V_read = sem("V_ps"), sem("V_read")
        split_done = sem("split_done")
        out_done, stored = sem("out_done"), sem("stored")
        unfit_done, unfit_ps, flag_done = sem("unfit_done"), sem("unfit_ps"), sem("flag_done")
        g_node_in, g_start, g_iota = sem("g_node_in"), sem("g_start"), sem("g_iota")
        g_freed, g_padded = sem("g_freed"), sem("g_padded")
        g_src, g_dst, g_e, g_src_seen = sem("g_src"), sem("g_dst"), sem("g_e"), sem("g_src_seen")
        g_got = [sem(f"g_got{g}") for g in range(2)]
        g_eT_ps, g_eT_sb, g_H_ps, g_pre, g_rows = (sem(n) for n in ("g_eT_ps", "g_eT_sb", "g_H_ps", "g_pre", "g_rows"))
        g_dst_sb, g_onehot, g_prod = sem("g_dst_sb"), sem("g_onehot"), sem("g_prod")
        g_aggT_ps, g_aggT_sb, g_z_ps, g_z_sb = (sem(n) for n in ("g_aggT_ps", "g_aggT_sb", "g_z_ps", "g_z_sb"))
        g_deg, g_sqrt, g_u, g_stored = (sem(n) for n in ("g_deg", "g_sqrt", "g_u", "g_stored"))

        PIECES = NB // PIECE
        X_PARTS = (slice(0, NB // 3), slice(NB // 3, NB * 2 // 3), slice(NB * 2 // 3, NB - 1))
        LOADS = 12
        x_blocks = x[0:(NB - 1) * P, :].rearrange("(b p) f -> p b f", p=P)
        out_blocks = out[0:(NB - 1) * P, :].rearrange("(b p) f -> p b f", p=P)

        def rows3(t):
            return t.rearrange("p (b c) -> p b c", c=GE)

        def nodes3(t):
            return t.rearrange("p (b f) -> p b f", f=F)

        def quad(t):
            return slice(QUAD * t, min(QUAD * t + QUAD, NB))

        def piece(t):
            return slice(PIECE * t, PIECE * t + PIECE)

        e_halves = edge[0:NFULL * GE, :].rearrange("(j k p g) f -> j p k g f", k=HALF, p=P, g=2)
        last_edges = slice(NFULL * GE, E)
        pairs = TAIL // 2
        STEP = NG + 1

        def if_unfit(eng):
            eng.wait_ge(flag_done, 1)
            is_unfit = eng.alloc_register("is_unfit")
            eng.load(is_unfit, flag[0:1, 0:1])
            return eng.If_ne(is_unfit, 0)

        block = ctx.enter_context(nc.Block())

        @block.sync
        def _(sp):
            sp.wait_ge(padded, 1)
            for part, landed in zip(X_PARTS, x_in):
                sp.dma_start(acc[:, part, :], x_blocks[:, part, :]).then_inc(landed, 16)
            sp.dma_start(acc[0:NLAST, NB - 1, :], x[(NB - 1) * P:N, :]).then_inc(x_in[-1], 16)
            sp.wait_ge(filled, 1)
            for dst_ap, src_ap in (
                    (W1n[0:F, 0:F], W1[0:F, :]), (W1n[F:, F:], W1[0:F, :]),
                    (W3n[0:F, 0:F], W3[0:F, :]), (W3n[F:, F:], W3[0:F, :]),
                    (b1_all, b1.unsqueeze(0).to_broadcast([P, F])), (b3_row[:, 0:F], b3.unsqueeze(0)), (b3_row[:, F:], b3.unsqueeze(0)),
                    (W1e[0:F, 0:F], W1[F:, :]), (W1e[F:, F:], W1[F:, :]),
                    (W2b[0:F, :], W2[:, :]), (W2b[F:F1, :], b2.unsqueeze(0)),
                    (W3a[:, :], W3[F:, :])):
                sp.dma_start(dst_ap, src_ap).then_inc(w_in, 16)

            def load_half(j, half):
                sp.dma_start(e_ring[:, HALF * half:HALF * half + HALF, :, :],
                             e_halves[j]).then_inc(e_in[half], 16)

            for i in range(3):
                sp.wait_ge(x_in[i], 16 if i < 2 else 32)
            sp.dma_start(x_dram[:, :, :], acc).then_inc(x_out, 16)

            P_blocks = P_dram.rearrange("(b p) f -> p b f", p=P)
            for t in range(QUADS):
                sp.wait_ge(P_sb, t + 1)
                sp.dma_start(P_blocks[:, quad(t), :], nodes3(P_s)[:, quad(t), :]).then_inc(P_out, 16)
            load_half(0, 0)
            load_half(1, 1)
            src_groups = src[0:NFULL * GE].rearrange("(n c) -> n c", c=GE)

            def load_src(k):
                sp.dma_start(src_all[:], src_groups[k].to_broadcast([P, GE])).then_inc(src_all_in, 16)

            load_src(slice(RING + ONE, RING + ONE + 1))
            sp.wait_ge(y3_sb, QUADS)
            sp.dma_start(y3_dram[:, :, :], nodes3(y3_s)).then_inc(y3_out, 16)

            def load_body(c, first):
                for j in range(BODY // HALF):
                    sp.wait_ge(eT_ps, c * BODY + (j * HALF + HALF))
                    load_half(c * (BODY // HALF) + (j + 2), j % 2)
                    if j == 0 and not first:
                        sp.wait_ge(squared, c * SETS)
                        sp.sem_inc(squared_seen, 1)
                        sp.wait_ge(hot_dve, c * SETS)
                        load_src(bass.ds(c * BODY + (RING + ONE), 1))

            sp.wait_ge(cleared[3], 1)
            sp.wait_ge(y3_ps, QUADS)
            for n in range(2):
                sp.dma_start(slab(ROWS + n), slab(NUMBERS + 5)).then_inc(copied_zeros, 16)

            load_body(0, True)
            with sp.Fori(1, NBODY) as c:
                load_body(c, False)
            sp.wait_ge(eT_ps, NFULL - RING + 1)
            last = edge[last_edges, :]
            sp.dma_start(e_ring[0:pairs, 0, :, :],
                         last[0:2 * pairs, :].rearrange("(p g) f -> p g f", g=2)).then_inc(last_in, 16)
            sp.wait_ge(last_in, 16)
            sp.dma_start(e_ring[pairs:pairs + 1, 0, 0, :], last[2 * pairs:TAIL, :]).then_inc(e_in[0], 16)
            sp.wait_ge(y3_out, 16)
            sp.wait_ge(x_out, 16)
            sp.wait_ge(H_ps, NFULL - 1)
            sp.dma_start(y3, y3_dram[:, :, :]).then_inc(y3_again, 16)
            sp.dma_start(acc, x_dram[:, :, :]).then_inc(x_again, 16)
            for t in range(PIECES):
                sp.wait_ge(out_done, t + 1)
                full = slice(PIECE * t, min(PIECE * t + PIECE, NB - 1))
                sp.dma_start(out_blocks[:, full, :], acc[:, full, :]).then_inc(stored, 16)
            sp.dma_start(out[(NB - 1) * P:N, :], acc[0:NLAST, NB - 1, :]).then_inc(stored, 16)
            sp.wait_ge(stored, 16 * (PIECES + 1))
            with if_unfit(sp):
                sp.wait_ge(g_start, 1)
                sp.dma_start(y3_g, y3_dram[:, :, :]).then_inc(g_node_in, 16)
                sp.dma_start(x2_g[:, 0:NB - 1, :], x_blocks).then_inc(g_node_in, 16)
                sp.dma_start(x2_g[0:NLAST, NB - 1, :], x[(NB - 1) * P:N, :]).then_inc(g_node_in, 16)
                for n in range(4):
                    with sp.Fori(0, NFULL) as k:
                        sp.wait_ge(g_freed, k + (n * NG + 1))
                        ks = bass.ds(k * GE, GE)
                        sp.dma_start(src_g, src[ks].rearrange("(p g) -> p g", g=2)).then_inc(g_src, 16)
                        sp.dma_start(dst_g, dst[ks].rearrange("(p g) -> p g", g=2)).then_inc(g_dst, 16)
                        if n == 0:
                            sp.dma_start(e_g, edge[ks, :].rearrange("(p g) f -> p g f", g=2)).then_inc(g_e, 16)
                    sp.wait_ge(g_padded, n + 1)
                    for flat, tile, landed in ((src, src_g, g_src), (dst, dst_g, g_dst)):
                        sp.dma_start(tile[0:pairs, :], flat[NFULL * GE:NFULL * GE + 2 * pairs].rearrange(
                            "(p g) -> p g", g=2)).then_inc(landed, 16)
                        sp.dma_start(tile[pairs:pairs + 1, 0:1], flat[E - 1:E].unsqueeze(0)).then_inc(landed, 16)
                    if n == 0:
                        sp.dma_start(e_g[0:pairs, :, :],
                                     last[0:2 * pairs, :].rearrange("(p g) f -> p g f", g=2)).then_inc(g_e, 16)
                        sp.dma_start(e_g[pairs:pairs + 1, 0, :], last[2 * pairs:TAIL, :]).then_inc(g_e, 16)
                    sp.wait_ge(g_u, n + 1)
                    if n < 3:
                        sp.dma_start(U_dram.rearrange("(b p) f -> p b f", p=P), u_g).then_inc(g_stored, 16)
                    else:
                        sp.dma_start(out_blocks, acc_g[:, 0:NB - 1, :]).then_inc(g_stored, 16)
                        sp.dma_start(out[(NB - 1) * P:N, :], acc_g[0:NLAST, NB - 1, :]).then_inc(g_stored, 16)
                sp.wait_ge(g_stored, 16 * 5)

        @block.gpsimd
        def _(pool):
            nc.gpsimd.memset(ident[:], 0.0).then_inc(consts, 1)
            pool.wait_ge(consts, 1)
            nc.gpsimd.affine_select(out=ident[:], in_=ident[:], compare_op=ALU.not_equal, fill=1.0,
                                    base=0, pattern=[[-1, P]], channel_multiplier=1).then_inc(consts, 1)
            nc.gpsimd.iota(iota_key[:], [[1, KEYS]], base=0, channel_multiplier=0,
                           allow_small_or_imprecise_dtypes=True)
            nc.gpsimd.iota(node_of, [[P, NB]], base=0, channel_multiplier=1,
                           allow_small_or_imprecise_dtypes=True).then_inc(consts, 1)
            nc.gpsimd.memset(A[:, 0:NUMBERS, :].bitcast(F32), 0.0).then_inc(cleared[0], 1)

            def gather(slot):
                for g in range(2):
                    nc.gpsimd.indirect_dma_start(
                        g_ring[:, slot, g, :], None, P_dram[:, :],
                        bass.IndirectOffsetOnAxis(ap=gidx[:, slot, g:g + 1], axis=0)
                    ).then_inc(gathered[slot], 16)

            pool.wait_ge(P_out, 16 * QUADS)
            pool.wait_ge(gidx_done, 1)
            for slot in range(RING):
                gather(slot)
            pool.wait_ge(turned_sb, 6)
            pool.wait_ge(wfold_sb, 2)
            nc.gpsimd.memset(slab(NUMBERS + 4), 0.0).then_inc(cleared[1], 1)
            with pool.Fori(0, NBODY) as c:
                for n, k in enumerate(k for k in range(BODY) if k != ONE):
                    pool.wait_ge(gidx_done, c * (BODY - 1) + (n + 2))
                    pool.sem_inc(gidx_seen, 1)
                    gather(k % RING)
            pool.wait_ge(gidx_done, NBODY * (BODY - 1) + 2)
            gather(0)

            def fetch(n, k, last_one):
                pool.wait_ge(g_src, 16 * STEP * (n + 1) if last_one else k * 16 + 16 * (STEP * n + 1))
                pool.sem_inc(g_src_seen, 1)
                for g in range(2):
                    nc.gpsimd.indirect_dma_start(
                        got_g[:, g, :], None, (P_dram if n == 0 else U_dram)[:, :],
                        bass.IndirectOffsetOnAxis(ap=src_g[:, g:g + 1], axis=0)).then_inc(g_got[g], 16)

            with if_unfit(pool):
                pool.wait_ge(g_start, 1)
                nc.gpsimd.iota(iota_g, [[1, NPAD]], base=0, channel_multiplier=0,
                               allow_small_or_imprecise_dtypes=True).then_inc(g_iota, 1)
                for n in range(4):
                    if n:
                        pool.wait_ge(g_stored, 16 * n)
                    with pool.Fori(0, NFULL) as k:
                        fetch(n, k, False)
                    fetch(n, NFULL, True)

        @block.scalar
        def _(act):
            act.wait_ge(padded, 1)
            for flat, tile, landed in ((src, src_s, src_in), (dst, dst_s, dst_in)):
                t3 = rows3(tile)
                act.dma_start(t3[:, 0:RB - 1, :],
                              flat[0:(RB - 1) * P * GE].rearrange("(b p c) -> p b c", p=P, c=GE)).then_inc(landed, 16)
                act.dma_start(t3[0:RLAST, RB - 1, :],
                              flat[(RB - 1) * P * GE:NFULL * GE].rearrange("(p c) -> p c", c=GE)).then_inc(landed, 16)
                act.dma_start(t3[RLAST:RLAST + 1, RB - 1, 0:TAIL],
                              flat[NFULL * GE:E].unsqueeze(0)).then_inc(landed, 16)
            act.wait_ge(src_in, 48)
            nc.scalar.copy(srcf_s, src_s).then_inc(srcf_done, 1)
            act.wait_ge(ln_var, 1)
            nc.scalar.activation(std, var, ACT.Sqrt, bias=epst[:, 0:1], scale=1.0 / F).then_inc(ln_std, 1)
            for g in range(2):
                act.wait_ge(src_turned, g + 1)
                nc.scalar.copy(srcT[:, :, g], ps[6 + g][:, 0:NFULL + RING]).then_inc(srcT_done, 1)

            act.wait_ge(srcT_done, 2)
            nc.scalar.copy(gidx[:, :, :], srcT[:, 0:RING, :]).then_inc(gidx_done, 1)

            for t in range(QUADS):
                act.wait_ge(hT_ps, t + 1)
                cols = slice(quad(t).start // 2 * P, -(-quad(t).stop // 2) * P)
                rows = P if quad(t).stop - quad(t).start > 1 else F
                nc.scalar.activation(hT[0:rows, cols], ps[t % 3][0:rows, 0:cols.stop - cols.start],
                                     ACT.Relu).then_inc(hT_sb, 1)
            act.wait_ge(ri_done, 1)
            nc.scalar.copy(rf_s, ri_s).then_inc(rf_done, 1)
            act.wait_ge(P_sb, QUADS)
            act.wait_ge(x_out, 16)
            nc.scalar.copy(P_parts[:, :, 0, :], nodes3(P_s)).then_inc(hi_P, 1)
            for t in range(QUADS):
                act.wait_ge(y3_ps, t + 1)
                n = quad(t).stop - quad(t).start
                nc.scalar.copy(nodes3(y3_s)[:, quad(t), :], nodes3(ps[t % 2][:, 0:n * F])).then_inc(y3_sb, 1)
            for i in range(6):
                act.wait_ge(turned, i + 1)
                tile = (rT, keyT, dlT)[i // 2]
                nc.scalar.copy(tile[:, :, i % 2], ps[2 + i][:, 0:NG]).then_inc(turned_sb, 1)
            act.wait_ge(rest_P, 1)
            nc.scalar.copy(P_parts[:, :, 1, :], nodes3(P_s)).then_inc(mid_P, 1)
            act.wait_ge(cleared[3], 1)
            zeros = slab(NUMBERS + 5)
            act.wait_ge(turned_sb, 6)
            for n in range(2):
                nc.scalar.copy(slab(NUMBERS + 2 + n), zeros).then_inc(cleared[2], 1)
            act.wait_ge(y3_out, 16)
            nc.scalar.copy(slab(24), zeros).then_inc(cleared[2], 1)
            act.wait_ge(parts_P, 1)
            nc.scalar.copy(slab(23), zeros).then_inc(cleared[2], 1)

            def edges_out(k, par, first):
                act.wait_ge(eT_ps, k + 1)
                if not first:
                    act.wait_ge(H_ps, k - 1)
                nc.scalar.copy(eT[:, par, :], ps_eT[:, 0:P]).then_inc(eT_sb, 1)

            def relu(k, par, third, first):
                act.wait_ge(H_ps, k + 1)
                if not first:
                    act.wait_ge(G_ps, k - 2)
                nc.scalar.activation(hid[:, third, :, 0:F],
                                     ps_H[par][:, 0:P].rearrange("p (g f) -> p g f", g=2),
                                     ACT.Relu).then_inc(hid_done, 1)

            def relu_one(c):
                act.wait_ge(part_sum, c + 2)
                rows = hid[:, ONE % 3, :, 0:F]
                nc.scalar.activation(rows, rows, ACT.Relu).then_inc(hid_done, 1)

            def numbers_ahead(k, slot):
                nc.scalar.copy(gidx[:, slot, :], srcT[:, bass.ds(k + RING, 1), :].rearrange(
                    "p k g -> p (k g)")).then_inc(gidx_done, 1)

            def hot_blocks(c, step):
                if step == 0:
                    act.wait_ge(src_all_in, c * 16 + 16)
                act.wait_ge(hot_used, c * SETS + max(step, 1))
                at = step % 2 * HOTS[0]
                q = step // 2 * sum(HOTS) + at
                many = HOTS[step % 2] - 1
                for n in range(many):
                    ins = nc.scalar.activation(oh_n[:, at + n, :, :], src_all[:].rearrange("p (c g) -> p g c", g=2),
                                               ACT.Square, bias=node_of[:, q + n:q + n + 1], scale=-1.0)
                ins.then_inc(squared, 1)
                act.wait_ge(squared, c * SETS + (step + 1))
                made = oh_n[:, at:at + many, :, :]
                nc.scalar.activation(made, made, ACT.Relu, bias=ones[:, 0:1], scale=-1.0).then_inc(hot_act, 1)

            edges_out(0, 0, True)
            for k in range(RING):
                edges_out(k + 1, (k + 1) % 2, k == 0)
                relu(k, k % 2, k % 3, k < 3)
                numbers_ahead(k, k)
            act.wait_ge(consts, 3)
            with act.Fori(0, NBODY) as c:
                for step in range(BODY):
                    k = c * BODY + (RING + step)
                    edges_out(k + 1, (step + 1) % 2, False)
                    if step < SETS:
                        hot_blocks(c, step)
                    if step == ONE + 1:
                        relu_one(c)
                    if step != ONE:
                        relu(k, step % 2, step % 3, False)
                    else:
                        act.wait_ge(H_ps, k + 1)
                    if (step + RING) % BODY != ONE:
                        numbers_ahead(k, step % RING)
            relu(NFULL, 0, 0, False)
            act.wait_ge(deg_done, 1)
            nc.scalar.activation(dis, dis, ACT.Sqrt).then_inc(sqrt_done, 1)
            act.wait_ge(ln_var, 2)
            nc.scalar.activation(std, var, ACT.Sqrt, bias=epst[:, 0:1], scale=1.0 / F).then_inc(ln_std, 1)
            for t in range(PIECES):
                act.wait_ge(u_done, t + 1)
                nc.scalar.copy(U[:, piece(t), 0, :], u_first[:, piece(t), :]).then_inc(hi_done, 1)
            for t in range(PIECES):
                act.wait_ge(r_done, t + 1)
                nc.scalar.copy(U[:, piece(t), 1, :], u_first[:, piece(t), :]).then_inc(mid_done, 1)
            for b in range(NB):
                ins = nc.scalar.activation(acc[:, b, :], acc[:, b, :], ACT.Relu, scale=rstd[:, b:b + 1])
            ins.then_inc(h2_done, 1)
            def hidden_rows(k):
                act.wait_ge(g_eT_ps, k + 1)
                nc.scalar.copy(eT_g, ps[5][:, 0:P]).then_inc(g_eT_sb, 1)
                act.wait_ge(g_pre, k + 1)
                nc.scalar.activation(rows_g[:, :, 0:F], pre_g, ACT.Relu).then_inc(g_rows, 1)

            with if_unfit(act):
                with act.Fori(0, NFULL) as k:
                    hidden_rows(k)
                hidden_rows(NFULL)
                act.wait_ge(ln_var, 3)
                nc.scalar.activation(std, var, ACT.Sqrt, bias=epst[:, 0:1], scale=1.0 / F).then_inc(ln_std, 1)
                act.wait_ge(g_deg, 1)
                nc.scalar.activation(dis, dis, ACT.Sqrt).then_inc(g_sqrt, 1)

        @block.tensor
        def _(pe):
            pe.wait_ge(consts, 2)

            def turn_numbers(i, tile, g, done):
                t4 = tile.rearrange("p (b c g) -> p b c g", g=2, c=P)
                for b in range(RB):
                    ins = pe.transpose(ps[i][:, b * P:b * P + P], t4[:, b, :, g], ident[:, :])
                ins.then_inc(done, 1)

            pe.wait_ge(srcf_done, 1)
            for g in range(2):
                turn_numbers(6 + g, srcf_s, g, src_turned)

            def turn_rows(t):
                pe.wait_ge(hn_done, t + 1)
                if t >= 3:
                    pe.wait_ge(hT_sb, t - 2)
                for n, b in enumerate(range(quad(t).start, quad(t).stop, 2)):
                    two = h_s[:, b * F:min(b + 2, NB) * F]
                    ins = pe.transpose(ps[t % 3][0:two.shape[1], n * P:n * P + P], two, ident[:, :])
                ins.then_inc(hT_ps, 1)

            def pairs_of(t):
                for n, b in enumerate(range(quad(t).start, quad(t).stop, 2)):
                    rows = P if b + 1 < NB else F
                    yield n, rows, hT[0:rows, b // 2 * P:b // 2 * P + P]

            def node_part(t):
                pe.wait_ge(hT_sb, t + 1)
                if t >= 3:
                    pe.wait_ge(P_sb, t - 2)
                for n, rows, turned_rows in pairs_of(t):
                    ins = pe.matmul(ps[3 + t % 3][:, n * P:n * P + rows], turned_rows, W1n[0:rows, 0:rows],
                                    start=True, stop=True)
                ins.then_inc(nodes_ps, 1)

            for t in range(QUADS):
                turn_rows(t)
                if t == 1:
                    pe.wait_ge(w_in, 16 * LOADS)
                if t >= 1:
                    node_part(t - 1)
            node_part(QUADS - 1)
            pe.wait_ge(filled, 1)
            for t in range(QUADS):
                if t >= 2:
                    pe.wait_ge(y3_sb, t - 1)
                for n, rows, turned_rows in pairs_of(t):
                    into = ps[t % 2][:, n * P:n * P + rows]
                    pe.matmul(into, turned_rows, W3n[0:rows, 0:rows], start=True, stop=False)
                    ins = pe.matmul(into, ones_row, b3_row[:, 0:rows], start=False, stop=True)
                ins.then_inc(y3_ps, 1)
            pe.wait_ge(P_sb, QUADS)
            pe.wait_ge(srcT_done, 2)
            pe.wait_ge(rf_done, 1)
            for g in range(2):
                turn_numbers(2 + g, rf_s, g, turned)
            pe.wait_ge(nat_done, 1)
            for i in range(2, 6):
                turn_numbers(2 + i, (key_s, dl_s)[i // 2 - 1], i % 2, turned)
            pe.wait_ge(y3_sb, QUADS)
            for b in range(RB):
                ins = pe.transpose(ps[1][0:1, b * P:b * P + P], base_n[:, b:b + 1], ident[:, :])
            ins.then_inc(base_turned, 1)
            pe.transpose(ps[0][0:F, 0:F1], W2b[:, :], ident[0:F1, 0:F1]).then_inc(wfold_ps, 1)
            pe.wait_ge(wfold_sb, 1)
            pe.matmul(ps[0][0:F1, 128:128 + F], W2T[:, :], W3a[:, :], start=True, stop=True).then_inc(wfold_ps, 1)
            pe.wait_ge(base_read, 1)
            pe.wait_ge(wfold_sb, 2)
            pe.wait_ge(turned_sb, 6)

            def turn(k, slot, first):
                if not first:
                    pe.wait_ge(eT_sb, k)
                pe.transpose(ps_eT[:, 0:P], e_ring[:, slot, :, :].rearrange("p g f -> p (g f)"),
                             ident[:, :]).then_inc(eT_ps, 1)

            def counts(k, par, first):
                pe.wait_ge(onehots, k + 1)
                if not first:
                    pe.wait_ge(A_added, k - 1)
                for g in range(2):
                    ins = pe.matmul(ps_A[par][:, 0:KEYS], oh_r[:, par, g, :], oh_key[:, par, g, :],
                                    start=(g == 0), stop=(g == 1))
                ins.then_inc(A_ps, 1)

            def hidden(landed, k, par, slot, first):
                pe.wait_ge(eT_sb, k + 1)
                if not first:
                    pe.wait_ge(hid_done, k - 1)
                pe.matmul(ps_H[par][:, 0:P], eT[:, par, :], W1e[:, :], start=True, stop=False)
                pe.wait_ge(gathered[slot], landed)
                pe.matmul(ps_H[par][:, 0:P], ident[:, :], g_ring[:, slot, :, :].rearrange("p g f -> p (g f)"),
                          start=False, stop=True).then_inc(H_ps, 1)

            def sums(k, par, third, first):
                pe.wait_ge(hid_done, k + 1)
                if not first:
                    pe.wait_ge(G_added, k - 1)
                for g in range(2):
                    ins = pe.matmul(ps_G[par][0:F1, 0:W], hid[:, third, g, :], oh_w[:, third, g, :],
                                    start=(g == 0), stop=(g == 1))
                ins.then_inc(G_ps, 1)

            def gather_blocks(c, step):
                pe.wait_ge(hot_act, c * SETS + (step + 1))
                pe.wait_ge(hot_dve, c * SETS + (step + 1))
                at = step % 2 * HOTS[0]
                for n in range(HOTS[step % 2]):
                    q = step // 2 * sum(HOTS) + at + n
                    for g in range(2):
                        ins = pe.matmul(ps_parts[:, g, 0:3, :].rearrange("p s f -> p (s f)"), oh_n[:, at + n, g, :],
                                        P_parts[:, q, :, :].rearrange("p s f -> p (s f)"),
                                        start=(q == 0 and g == 0), stop=False)
                ins.then_inc(hot_used, 1)

            def hidden_one(k, par):
                pe.wait_ge(eT_sb, k + 1)
                pe.matmul(ps_parts[:, :, 3, :], eT[:, par, :], W1e[:, :], start=False, stop=True).then_inc(H_ps, 1)

            pe.wait_ge(e_in[0], 16)
            turn(0, 0, True)
            for k in range(RING):
                if k + 1 == HALF:
                    pe.wait_ge(e_in[1], 16)
                if k + 1 == RING:
                    pe.wait_ge(e_in[0], 16 * 2)
                turn(k + 1, (k + 1) % RING, False)
                if k >= 2:
                    sums(k - 2, k % 2, (k - 2) % 3, k < 4)
                counts(k, k % 2, k < 2)
                hidden(16 * 2, k, k % 2, k, k < 2)
            pe.wait_ge(parts_P, 1)
            pe.sem_inc(hot_used, 1)
            with pe.Fori(0, NBODY) as c:
                for step in range(BODY):
                    k, slot = c * BODY + (RING + step), step % RING
                    ahead = step + 1
                    if ahead % HALF == 0:
                        pe.wait_ge(e_in[ahead % RING // HALF], c * (16 * BODY // RING) + 16 * (ahead // RING + 2))
                    turn(k + 1, ahead % RING, False)
                    sums(k - 2, step % 2, (step - 2) % 3, False)
                    counts(k, step % 2, False)
                    if step == 1:
                        pe.wait_ge(part_sum, c + 1)
                    if 1 <= step <= SETS:
                        gather_blocks(c, step - 1)
                    if step == ONE:
                        hidden_one(k, step % 2)
                    else:
                        per_body = BODY // RING - (slot == ONE % RING)
                        hidden(c * (32 * per_body) + 32 * (step // RING + 2), k, step % 2, slot, False)
            sums(NFULL - 2, 0, 1, False)
            counts(NFULL, 0, False)
            hidden(32 * (NFULL // RING + 1), NFULL, 0, 0, False)
            sums(NFULL - 1, 1, 2, False)
            sums(NFULL, 0, 0, False)
            pe.wait_ge(A_added, NG)
            pe.wait_ge(G_added, NG)
            for t in range(PIECES):
                for j in range(PIECE):
                    b = t * PIECE + j
                    ins = pe.matmul(ps[t][:, j * F1:(j + 1) * F1], aggT[:, b * P:b * P + P],
                                    W23[:, :], start=True, stop=True)
                ins.then_inc(z_ps, 1)
            with pe.Fori(0, LAYERS) as layer:
                for b in range(NB):
                    pe.wait_ge(V_read, layer * NB + (b + 1))
                    for q in range(NB):
                        if b == 0 and q % PIECE == 0:
                            pe.wait_ge(U_done, layer * PIECES + (q // PIECE + 1))
                        ins = pe.matmul(ps[b % PIECE][:, 0:3 * F], A[:, q, b * P:b * P + P],
                                        U[:, q, :, :].rearrange("p s f -> p (s f)"),
                                        start=(q == 0), stop=(q == NB - 1))
                    ins.then_inc(V_ps, 1)
            pe.wait_ge(unfit_done, 1)
            pe.matmul(ps[5][0:1, 0:1], unfit[:, 0:1], ones[:, :], start=True, stop=True).then_inc(unfit_ps, 1)

            def scatter(n, k, last_one):
                if n == 0:
                    pe.wait_ge(g_e, 16 * STEP if last_one else k * 16 + 16)
                    pe.transpose(ps[5][:, 0:P], e_g.rearrange("p g f -> p (g f)"), ident[:, :]).then_inc(g_eT_ps, 1)
                    pe.wait_ge(g_eT_sb, k + 1)
                    pe.matmul(ps[6][:, 0:P], eT_g, W1e[:, :], start=True, stop=True).then_inc(g_H_ps, 1)
                    pe.wait_ge(g_rows, k + 1)
                else:
                    for g in range(2):
                        pe.wait_ge(g_got[g], k * 16 + 16 * (NG * n + 1))
                pe.wait_ge(g_onehot, k + (NG * n + 1))
                width = F1 if n == 0 else F
                for b in range(NB):
                    at = b % PIECE * F1
                    for g in range(2):
                        ins = pe.matmul(ps[b // PIECE][:, at:at + width], oh_g[:, g, b * P:b * P + P],
                                        (rows_g if n == 0 else got_g)[:, g, :], start=(g == 0), stop=(g == 1))
                ins.then_inc(g_prod, 1)

            with if_unfit(pe):
                for n in range(4):
                    with pe.Fori(0, NFULL) as k:
                        scatter(n, k, False)
                    scatter(n, NFULL, True)
                    if n == 0:
                        pe.wait_ge(g_freed, NG + 1)
                        for b in range(NB):
                            pe.transpose(ps[5][0:F1, 0:P], sums_g[:, b, :], ident[:, :]).then_inc(g_aggT_ps, 1)
                            pe.wait_ge(g_aggT_sb, b + 1)
                            pe.matmul(ps[6][:, 0:F1], aggT[:, b * P:b * P + P], W23[:, :],
                                      start=True, stop=True).then_inc(g_z_ps, 1)
                            pe.wait_ge(g_z_sb, b + 1)

        @block.vector
        def _(dve):
            chain = [0]

            def link(ins):
                chain[0] += 1
                ins.then_inc(link_d, 1)
                dve.wait_ge(link_d, chain[0])

            def per_node(t, n=NB):
                return t.unsqueeze(2).to_broadcast([P, n, F])

            nc.vector.memset(acc[:, NB - 1, :], 0.0)
            nc.vector.memset(rows3(src_s)[:, RB - 1, :], 0)
            nc.vector.memset(rows3(dst_s)[:, RB - 1, :], FAR).then_inc(padded, 1)
            nc.vector.memset(epst[:], EPS)
            nc.vector.memset(W1e[:], 0.0)
            nc.vector.memset(after_hT[:, 0:2 * P], 0.0)
            nc.vector.memset(ones[:], 1.0)
            nc.vector.memset(hid[:], 1.0)
            nc.vector.memset(ones_row, 1.0)
            link(nc.vector.memset(W23[:], 0.0))
            nc.vector.memset(W23[F:F1, F:F1], 1.0).then_inc(filled, 1)
            nc.vector.memset(slab(NUMBERS + 5), 0.0).then_inc(cleared[3], 1)
            nc.vector.memset(aggT[:], 0.0)

            def deviations(n, bn, meanwhile=None):
                nc.vector.tensor_tensor(mean, bn[:, :, 1], bn[:, :, 4], ALU.add)
                nc.vector.tensor_tensor(var, bn[:, :, 2], bn[:, :, 5], ALU.add)
                link(nc.vector.tensor_tensor(gap, bn[:, :, 1], bn[:, :, 4], ALU.subtract))
                nc.vector.tensor_scalar(mean, mean, 0.5, None, ALU.mult)
                link(nc.vector.scalar_tensor_tensor(out=gap, in0=gap, scalar=F / 4.0, in1=gap,
                                                    op0=ALU.mult, op1=ALU.mult))
                nc.vector.tensor_tensor(var, var, gap, ALU.add).then_inc(ln_var, 1)
                if meanwhile:
                    meanwhile()
                dve.wait_ge(ln_std, n)
                link(nc.vector.reciprocal(rstd, std))

            for i, part in enumerate(X_PARTS):
                dve.wait_ge(x_in[i], 16 if i < 2 else 32)
                for b in range(part.start, part.stop + (i == 2)):
                    ins = nc.vector.bn_stats(bn_start[:, b, :], acc[:, b, :])
            link(ins)
            deviations(1, bn_start)

            def centre(t):
                n = quad(t).stop - quad(t).start
                nc.vector.tensor_tensor(nodes3(h_s)[:, quad(t), :], acc[:, quad(t), :],
                                        per_node(mean[:, quad(t)], n), ALU.subtract).then_inc(hn_sub, 1)

            centre(0)
            for t in range(QUADS):
                if t + 1 < QUADS:
                    centre(t + 1)
                dve.wait_ge(hn_sub, t + 1)
                part = nodes3(h_s)[:, quad(t), :]
                nc.vector.tensor_tensor(part, part, per_node(rstd[:, quad(t)], quad(t).stop - quad(t).start),
                                        ALU.mult).then_inc(hn_done, 1)
            dve.wait_ge(src_in, 48)
            nc.vector.tensor_scalar(ri_s, src_s, P - 1, None, ALU.bitwise_and).then_inc(ri_done, 1)
            dve.wait_ge(dst_in, 48)
            link(nc.vector.tensor_reduce(base_n[:], rows3(dst_s), AX.X, ALU.min))
            for t in range(QUADS):
                dve.wait_ge(nodes_ps, t + 1)
                n = quad(t).stop - quad(t).start
                nc.vector.tensor_tensor(nodes3(P_s)[:, quad(t), :], nodes3(ps[3 + t % 3][:, 0:n * F]),
                                        b1_all.unsqueeze(1).to_broadcast([P, n, F]), ALU.add).then_inc(P_sb, 1)
            link(nc.vector.tensor_tensor(rows3(key_s), rows3(dst_s),
                                         base_n[:].unsqueeze(2).to_broadcast([P, RB, GE]), ALU.subtract))
            link(nc.vector.tensor_scalar(dl_s, key_s, W - 0.5, NO_SLOT, ALU.is_gt, ALU.mult))
            nc.vector.tensor_reduce(unfit[:, 0:1], dl_s, AX.X, ALU.add)
            dve.wait_ge(rf_done, 1)
            link(nc.vector.scalar_tensor_tensor(out=dl_s, in0=key_s, scalar=NO_SLOT, in1=dl_s,
                                                op0=ALU.min, op1=ALU.max))
            link(nc.vector.tensor_tensor(key_s, srcf_s, rf_s, ALU.subtract))
            nc.vector.scalar_tensor_tensor(out=key_s, in0=key_s, scalar=float(W) / P, in1=dl_s,
                                           op0=ALU.mult, op1=ALU.add).then_inc(nat_done, 1)
            dve.wait_ge(P_out, 16 * QUADS)
            dve.wait_ge(hi_P, 1)
            nc.vector.tensor_tensor(nodes3(P_s), nodes3(P_s), P_parts[:, :, 0, :], ALU.subtract).then_inc(rest_P, 1)
            dve.wait_ge(base_turned, 1)
            nc.vector.tensor_copy(base_row[:], ps[1][0:1, :]).then_inc(base_read, 1)
            dve.wait_ge(wfold_ps, 1)
            nc.vector.tensor_copy(W2T[:, :], ps[0][0:F, 0:F1]).then_inc(wfold_sb, 1)
            dve.wait_ge(wfold_ps, 2)
            nc.vector.tensor_copy(W23[:, 0:F], ps[0][0:F1, 128:128 + F]).then_inc(wfold_sb, 1)
            dve.wait_ge(turned_sb, 6)
            link(nc.vector.memset(slab(NUMBERS, 2), 0.0))
            dve.wait_ge(mid_P, 1)
            nc.vector.tensor_tensor(P_parts[:, :, 2, :], nodes3(P_s), P_parts[:, :, 1, :], ALU.subtract).then_inc(parts_P, 1)
            dve.wait_ge(consts, 3)
            dve.wait_ge(base_read, 1)

            def make_onehots(k, par, third, first):
                if not first:
                    dve.wait_ge(G_ps, k - 2)
                if not first or third == 2:
                    dve.wait_ge(A_ps, k - 1)
                nc.vector.tensor_tensor(
                    oh_w[:, third, :, :], iota_w.unsqueeze(1).to_broadcast([P, 2, W]),
                    dlT[:, bass.ds(k, 1), :].rearrange("p k g -> p (k g)").unsqueeze(2).to_broadcast([P, 2, W]),
                    ALU.is_equal)
                for g in range(2):
                    nc.vector.tensor_scalar(oh_r[:, par, g, :], iota_r,
                                            rT[:, bass.ds(k, 1), g], None, ALU.is_equal)
                    ins = nc.vector.tensor_scalar(oh_key[:, par, g, :], iota_key[:],
                                                  keyT[:, bass.ds(k, 1), g], None, ALU.is_equal)
                ins.then_inc(onehots, 1)

            def add_counts(k, par, base, first):
                dve.wait_ge(A_ps, k + 1)
                if first:
                    dve.wait_ge(cleared[0], 1)
                    dve.wait_ge(cleared[1], 1)
                    dve.wait_ge(cleared[2], 4)
                    dve.wait_ge(copied_zeros, 32)
                else:
                    dve.wait_ge(A_added, k)
                Aw = A[:, :, bass.ds(base, W)]
                nc.vector.tensor_tensor(Aw, Aw, ps_A[par][:, 0:KEYS].rearrange("p (q w) -> p q w", w=W),
                                        ALU.add).then_inc(A_added, 1)

            def add_sums(k, par, base, first):
                dve.wait_ge(G_ps, k + 1)
                if not first:
                    dve.wait_ge(G_added, k)
                Gw = aggT[:, bass.ds(base, W)]
                nc.vector.tensor_tensor(Gw, Gw, ps_G[par][0:F1, 0:W], ALU.add).then_inc(G_added, 1)

            def load_bases(k, n):
                _, vals = nc.values_load_multi_w_load_instructions(
                    base_row[0:1, bass.ds(k, n)], engines=[mybir.EngineType.DVE], min_val=0, max_val=NPAD - W,
                    skip_runtime_bounds_check_because="a destination is below N, and N - 1 + W is within the padded width")
                return vals

            def hot_block(c, step):
                if step == 0:
                    dve.wait_ge(src_all_in, c * 16 + 16)
                dve.wait_ge(hot_used, c * SETS + max(step, 1))
                at = step % 2 * HOTS[0] + HOTS[step % 2] - 1
                q = step // 2 * sum(HOTS) + at
                nc.vector.tensor_scalar(oh_n[:, at, :, :], src_all[:].rearrange("p (c g) -> p g c", g=2),
                                        node_of[:, q:q + 1], None, ALU.is_equal).then_inc(hot_dve, 1)

            def sum_parts(k):
                dve.wait_ge(H_ps, k + 1)
                nc.vector.tensor_reduce(hid[:, ONE % 3, :, 0:F], ps_parts.rearrange("p g s f -> p g f s"),
                                        AX.X, ALU.add).then_inc(part_sum, 1)

            vals = load_bases(0, RING)
            for k in range(RING):
                make_onehots(k, k % 2, k % 3, k < 3)
                if k >= 1:
                    add_counts(k - 1, (k + 1) % 2, vals[k - 1], k == 1)
                if k >= 2:
                    add_sums(k - 2, k % 2, vals[k - 2], k == 2)
            dve.sem_inc(part_sum, 1)
            with dve.Fori(0, NBODY) as c:
                for step in range(BODY):
                    k = c * BODY + (RING + step)
                    if step % RING == 0:
                        vals = load_bases(k - 2, RING + 2)
                    slot = step % RING
                    make_onehots(k, step % 2, step % 3, False)
                    if step == ONE + 1:
                        sum_parts(k - 1)
                    add_counts(k - 1, (step + 1) % 2, vals[slot + 1], False)
                    add_sums(k - 2, step % 2, vals[slot], False)
                    if step < SETS:
                        hot_block(c, step)
            vals = load_bases(NFULL - 2, 3)
            make_onehots(NFULL, 0, 0, False)
            add_counts(NFULL - 1, 1, vals[1], False)
            add_sums(NFULL - 2, 0, vals[0], False)
            add_counts(NFULL, 0, vals[2], False)
            add_sums(NFULL - 1, 1, vals[1], False)
            add_sums(NFULL, 0, vals[2], False)
            dve.wait_ge(y3_again, 16)
            dve.wait_ge(x_again, 16)

            def update_sum(t):
                dve.wait_ge(z_ps, t + 1)
                z = ps[t][:, 0:PIECE * F1].rearrange("p (j c) -> p j c", c=F1)
                nc.vector.tensor_copy(deg[:, piece(t)], z[:, :, F])
                nc.vector.tensor_tensor(y3[:, piece(t), :], y3[:, piece(t), :], z[:, :, 0:F],
                                        ALU.add).then_inc(V_read, 1)

            def residual(t):
                dve.wait_ge(V_read, t + 1)
                nc.vector.scalar_tensor_tensor(out=y3[:, piece(t), :], in0=y3[:, piece(t), :], scalar=0.0,
                                               in1=acc[:, piece(t), :], op0=ALU.max, op1=ALU.add).then_inc(x2_sum, 1)

            update_sum(0)
            for t in range(PIECES):
                if t + 1 < PIECES:
                    update_sum(t + 1)
                residual(t)
                if t + 1 == PIECES:
                    nc.vector.tensor_scalar(dis, deg, 1.0, None, ALU.max).then_inc(deg_done, 1)
                dve.wait_ge(x2_sum, t + 1)
                for b in range(PIECE * t, PIECE * t + PIECE):
                    ins = nc.vector.bn_stats(bn_later[:, b, :], y3[:, b, :])
            link(ins)

            def centre_all():
                for t in range(PIECES):
                    nc.vector.tensor_tensor(acc[:, piece(t), :], y3[:, piece(t), :],
                                            per_node(mean[:, piece(t)], PIECE), ALU.subtract).then_inc(xc_done, 1)

            deviations(2, bn_later, centre_all)
            dve.wait_ge(sqrt_done, 1)
            link(nc.vector.reciprocal(dis, dis))
            link(nc.vector.scalar_tensor_tensor(out=dis, in0=deg, scalar=0.5, in1=dis, op0=ALU.is_gt, op1=ALU.mult))
            nc.vector.tensor_tensor(dis2, dis, dis, ALU.mult)
            link(nc.vector.tensor_tensor(gap, dis, rstd, ALU.mult))
            for t in range(PIECES):
                dve.wait_ge(xc_done, t + 1)
                nc.vector.scalar_tensor_tensor(out=u_first[:, piece(t), :], in0=acc[:, piece(t), :], scalar=0.0,
                                               in1=per_node(gap[:, piece(t)], PIECE),
                                               op0=ALU.max, op1=ALU.mult).then_inc(u_done, 1)
            for t in range(PIECES):
                dve.wait_ge(hi_done, t + 1)
                nc.vector.tensor_tensor(u_first[:, piece(t), :], u_first[:, piece(t), :], U[:, piece(t), 0, :],
                                        ALU.subtract).then_inc(r_done, 1)
            for t in range(PIECES):
                dve.wait_ge(mid_done, t + 1)
                nc.vector.tensor_tensor(U[:, piece(t), 2, :], u_first[:, piece(t), :], U[:, piece(t), 1, :],
                                        ALU.subtract).then_inc(U_done, 1)
            link(nc.vector.tensor_scalar(mean, deg, MAX_EXACT + 0.5, NO_SLOT, ALU.is_gt, ALU.mult))
            link(nc.vector.tensor_reduce(unfit[:, 1:2], mean, AX.X, ALU.add))
            nc.vector.tensor_tensor(unfit[:, 0:1], unfit[:, 0:1], unfit[:, 1:2], ALU.add).then_inc(unfit_done, 1)
            dve.wait_ge(h2_done, 1)

            def read_product(layer, b):
                dve.wait_ge(V_ps, layer * NB + (b + 1))
                nc.vector.tensor_reduce(v[:, b % 2, :], ps[b % PIECE][:, 0:3 * F].rearrange(
                    "p (s f) -> p f s", f=F), AX.X, ALU.add).then_inc(V_read, 1)
                dve.wait_ge(V_read, layer * NB + (b + 1 + PIECES))
                return nc.vector.scalar_tensor_tensor(out=acc[:, b, :], in0=v[:, b % 2, :], scalar=dis[:, b:b + 1],
                                                      in1=acc[:, b, :], op0=ALU.mult, op1=ALU.add)

            def split_next(layer, b):
                def step(i, ins):
                    ins.then_inc(split_done, 1)
                    dve.wait_ge(split_done, layer * (NB * SPLIT_STEPS) + (b * SPLIT_STEPS + i))
                vb, rb, scale = v[:, b % 2, :], rem[:, b % 2, :], dis2[:, b:b + 1]
                hi, mid, lo = (U_next[:, b, s, :] for s in range(3))
                step(1, nc.vector.tensor_scalar(hi, vb, scale, None, ALU.mult))
                step(2, nc.vector.scalar_tensor_tensor(out=rb, in0=vb, scalar=scale, in1=hi,
                                                       op0=ALU.mult, op1=ALU.subtract))
                step(3, nc.vector.tensor_copy(mid, rb))
                step(4, nc.vector.tensor_tensor(lo, rb, mid, ALU.subtract))

            def hand_over(t):
                nc.vector.tensor_copy(U[:, piece(t), :, :], U_next[:, piece(t), :, :]).then_inc(U_done, 1)

            with dve.Fori(0, LAYERS - 1) as layer:
                for b in range(NB - 1):
                    read_product(layer, b)
                    split_next(layer, b)
                read_product(layer, NB - 1)
                for t in range(PIECES - 1):
                    hand_over(t)
                split_next(layer, NB - 1)
                hand_over(PIECES - 1)
            for b in range(NB):
                ins = read_product(LAYERS - 1, b)
                if b % PIECE == PIECE - 1:
                    t = b // PIECE
                    link(ins)
                    nc.vector.scalar_tensor_tensor(out=acc[:, piece(t), :], in0=acc[:, piece(t), :], scalar=0.25,
                                                   in1=y3[:, piece(t), :], op0=ALU.mult,
                                                   op1=ALU.add).then_inc(out_done, 1)
            dve.wait_ge(unfit_ps, 1)
            nc.vector.tensor_scalar(flag[:], ps[5][0:1, 0:1], NO_SLOT * (GE - TAIL + 0.5), None,
                                    ALU.is_gt).then_inc(flag_done, 1)

            def general():
                link(nc.vector.memset(rows_g, 1.0))
                link(nc.vector.memset(x2_g[:, NB - 1, :], 0.0))
                link(nc.vector.memset(sums_g, 0.0))
                nc.vector.engine_nop().then_inc(g_start, 1)
                nc.vector.engine_nop().then_inc(g_freed, 1)
                dve.wait_ge(g_iota, 1)

                def onehot_and_sum(n, k, last_one):
                    dve.wait_ge(g_dst, 16 * STEP * (n + 1) if last_one else k * 16 + 16 * (STEP * n + 1))
                    nc.vector.tensor_copy(dstf_g, dst_g).then_inc(g_dst_sb, 1)
                    dve.wait_ge(g_dst_sb, k + (n * NG + 1))
                    for g in range(2):
                        ins = nc.vector.tensor_scalar(oh_g[:, g, :], iota_g, dstf_g[:, g:g + 1], None, ALU.is_equal)
                    ins.then_inc(g_onehot, 1)
                    if n == 0:
                        dve.wait_ge(g_H_ps, k + 1)
                        for g in range(2):
                            dve.wait_ge(g_got[g], k * 16 + 16)
                        nc.vector.tensor_tensor(pre_g, ps[6][:, 0:P].rearrange("p (g f) -> p g f", g=2),
                                                got_g, ALU.add).then_inc(g_pre, 1)
                    width = F1 if n == 0 else F
                    dve.wait_ge(g_prod, k + (n * NG + 1))
                    for t in range(NB // PIECE):
                        part = ps[t][:, 0:PIECE * F1].rearrange("p (j c) -> p j c", c=F1)[:, :, 0:width]
                        into = sums_g[:, t * PIECE:(t + 1) * PIECE, 0:width]
                        ins = nc.vector.tensor_tensor(into, into, part, ALU.add)
                    ins.then_inc(g_freed, 1)
                    dve.wait_ge(g_freed, k + (n * NG + 2))

                for n in range(4):
                    with dve.Fori(0, NFULL) as k:
                        onehot_and_sum(n, k, False)
                    nc.vector.memset(src_g, 0)
                    nc.vector.memset(e_g, 0.0)
                    nc.vector.memset(dst_g, FAR).then_inc(g_padded, 1)
                    onehot_and_sum(n, NFULL, True)
                    if n == 0:
                        dve.wait_ge(g_node_in, 48)
                        for b in range(NB):
                            dve.wait_ge(g_aggT_ps, b + 1)
                            nc.vector.tensor_copy(aggT[:, b * P:b * P + P], ps[5][0:F1, 0:P]).then_inc(g_aggT_sb, 1)
                            dve.wait_ge(g_z_ps, b + 1)
                            nc.vector.tensor_copy(deg[:, b:b + 1], ps[6][:, F:F1])
                            nc.vector.tensor_tensor(y3_g[:, b, :], y3_g[:, b, :], ps[6][:, 0:F],
                                                    ALU.add).then_inc(g_z_sb, 1)
                        dve.wait_ge(g_z_sb, NB)
                        nc.vector.tensor_scalar(dis, deg, 1.0, None, ALU.max).then_inc(g_deg, 1)
                        link(nc.vector.scalar_tensor_tensor(out=x2_g, in0=y3_g, scalar=0.0, in1=x2_g,
                                                            op0=ALU.max, op1=ALU.add))
                        for b in range(NB):
                            ins = nc.vector.bn_stats(bn_later[:, b, :], x2_g[:, b, :])
                        link(ins)
                        deviations(3, bn_later)
                        link(nc.vector.tensor_tensor(acc_g, x2_g, per_node(mean), ALU.subtract))
                        link(nc.vector.scalar_tensor_tensor(out=acc_g, in0=acc_g, scalar=0.0, in1=per_node(rstd),
                                                            op0=ALU.max, op1=ALU.mult))
                        dve.wait_ge(g_sqrt, 1)
                        link(nc.vector.reciprocal(dis, dis))
                        link(nc.vector.scalar_tensor_tensor(out=dis, in0=deg, scalar=0.5, in1=dis,
                                                            op0=ALU.is_gt, op1=ALU.mult))
                        nc.vector.tensor_tensor(u_g, acc_g, per_node(dis), ALU.mult).then_inc(g_u, 1)
                    else:
                        link(nc.vector.tensor_tensor(sq_g, sums_g[:, :, 0:F], per_node(dis), ALU.mult))
                        link(nc.vector.tensor_tensor(acc_g, acc_g, sq_g, ALU.add))
                        if n < 3:
                            dve.wait_ge(g_stored, 16 * n)
                            nc.vector.tensor_tensor(u_g, sq_g, per_node(dis), ALU.mult).then_inc(g_u, 1)
                        else:
                            nc.vector.scalar_tensor_tensor(out=acc_g, in0=acc_g, scalar=0.25, in1=x2_g,
                                                           op0=ALU.mult, op1=ALU.add).then_inc(g_u, 1)
                    if n < 3:
                        link(nc.vector.memset(sums_g, 0.0))

            with if_unfit(dve):
                general()


_INS = ['x', 'src', 'dst', 'edge_attr_64', 'L0_gnn_W1', 'L0_gnn_b1', 'L0_gnn_W2', 'L0_gnn_b2', 'L0_gnn_W3', 'L0_gnn_b3']


def kernel(**inputs):
    import numpy as _np
    import concourse.bacc as _bacc
    from concourse import mybir as _mybir
    from concourse.bass_utils import run_bass_kernel_spmd as _run

    nc = _bacc.Bacc("TRN2", target_bir_lowering=False, num_devices=1)
    arrays, args = {}, []
    for name in _INS:
        a = _np.ascontiguousarray(inputs[name])
        arrays[f"in_{name}_dram"] = a
        args.append(nc.dram_tensor(f"in_{name}_dram", a.shape, _mybir.dt.from_np(a.dtype), kind="ExternalInput").ap())
    args.append(nc.dram_tensor("out_0_dram", inputs['x'].shape, F32, kind="ExternalOutput").ap())
    gnn_and_propagation(nc, *args)
    r = _run(nc, [arrays], core_ids=[0])
    return r.results[0]["out_0_dram"]
```
